# Optimizing a Trainium2 kernel written in Bass

```python
import numpy as np
import jax
import jax.numpy as jnp

def _softmax(x, axis=-1):
    return jax.nn.softmax(x, axis=axis)

def _gelu(x):
    return jax.nn.gelu(x, approximate=True)

def _silu(x):
    return jax.nn.silu(x)

def _sigmoid(x):
    return jax.nn.sigmoid(x)

def _layernorm(x, axis=-1, eps=1e-05):
    m = jnp.mean(x, axis=axis, keepdims=True)
    v = jnp.var(x, axis=axis, keepdims=True)
    return (x - m) / jnp.sqrt(v + eps)

def _scatter_add(tgt, idx, src, axis=0):
    return tgt.at[idx].add(src)

def _segment_sum(src, seg, n):
    return jax.ops.segment_sum(src, seg, n)
kernel_name = 'mk_pixart_seq_d1_seqx_r2_222b25'

def setup_inputs(seed: int=0):
    np.random.seed(seed)
    _w = jnp.asarray

    def _rec_inputs():
        import jax
        import jax.numpy as jnp
        _rk = jax.random.key(seed)
        x = -0.0002928 + 1 * jax.random.normal(jax.random.fold_in(_rk, 1), (16, 256, 512), jnp.float32)
        _lenS = 256 - jax.random.randint(jax.random.fold_in(_rk, 7), (16,), 0, max(1, 256 // 4) + 1, jnp.int32)
        _lenS2 = 256 - jax.random.randint(jax.random.fold_in(_rk, 8), (16,), 0, max(1, 256 // 4) + 1, jnp.int32)
        cond_1024 = 0.000887014 + 1.03683 * jax.random.normal(jax.random.fold_in(_rk, 11), (16, 512), jnp.float32)
        _ctx_1024P = jax.random.normal(jax.random.fold_in(_rk, 12), (16, 16, 512), jnp.float32)
        _ctx_1024c = jax.random.dirichlet(jax.random.fold_in(_rk, 512), 0.3 * jnp.ones((16,), jnp.float32), (16, 256))
        _ctx_1024t = jnp.einsum('bsk,bkd->bsd', _ctx_1024c, _ctx_1024P)
        _ctx_1024t = _ctx_1024t * jax.lax.rsqrt(jnp.mean(jnp.square(_ctx_1024t)) + 1e-12) * 0.953939
        ctx_1024 = 0.00086875 + 0.999764 * (_ctx_1024t + 0.3 * jax.random.normal(jax.random.fold_in(_rk, 612), (16, 256, 512), jnp.float32))
        return (x, cond_1024, ctx_1024)
    x, cond_1024, ctx_1024 = _rec_inputs()

    def _L0_xcond_setup():
        import jax, jax.numpy as jnp
        import numpy as np
        import math
        D_MODEL = 512
        N_HEADS = 16
        HEAD_DIM = D_MODEL // N_HEADS
        D_FF = 2048
        EPS = 1e-05
        ROPE_BASE = 10000.0

        def _rope(t):
            L, Dh = (t.shape[1], t.shape[-1])
            half = Dh // 2
            inv_freq = 1.0 / ROPE_BASE ** (jnp.arange(half, dtype=t.dtype) / half)
            ang = jnp.arange(L, dtype=t.dtype)[:, None] * inv_freq[None, :]
            cos = jnp.cos(ang)[None, :, None, :]
            sin = jnp.sin(ang)[None, :, None, :]
            t1, t2 = (t[..., :half], t[..., half:])
            return jnp.concatenate([t1 * cos - t2 * sin, t2 * cos + t1 * sin], axis=-1)

        def _adaln(x, emb, w, b):
            e = emb[:, 0, :]
            gb = e @ w.T + b
            gamma, beta = jnp.split(gb, 2, axis=-1)
            mu = x.mean(-1, keepdims=True)
            var = x.var(-1, keepdims=True)
            xn = (x - mu) * jax.lax.rsqrt(var + EPS)
            return xn * (1.0 + gamma[:, None, :]) + beta[:, None, :]

        def _attn(q, k, v):
            scale = 1.0 / math.sqrt(HEAD_DIM)
            scores = jnp.einsum('bqhd,bkhd->bhqk', q, k) * scale
            w = jax.nn.softmax(scores, axis=-1)
            out = jnp.einsum('bhqk,bkhd->bqhd', w, v)
            B, Lq = (out.shape[0], out.shape[1])
            return out.reshape(B, Lq, D_MODEL)
        key = jax.random.key(seed)
        ks = jax.random.split(key, 24)
        s = 0.02
        inp = {'x': jax.random.normal(ks[0], (2, 1024, D_MODEL), jnp.float32), 'noise_emb': jax.random.normal(ks[1], (2, 1, D_MODEL), jnp.float32), 'context': jax.random.normal(ks[2], (2, 512, D_MODEL), jnp.float32), 'ln1_w': jax.random.normal(ks[3], (2 * D_MODEL, D_MODEL), jnp.float32) * s, 'ln1_b': jax.random.normal(ks[4], (2 * D_MODEL,), jnp.float32) * s, 'ln2_w': jax.random.normal(ks[5], (2 * D_MODEL, D_MODEL), jnp.float32) * s, 'ln2_b': jax.random.normal(ks[6], (2 * D_MODEL,), jnp.float32) * s, 'ln3_w': jax.random.normal(ks[7], (2 * D_MODEL, D_MODEL), jnp.float32) * s, 'ln3_b': jax.random.normal(ks[8], (2 * D_MODEL,), jnp.float32) * s, 'qkv_w': jax.random.normal(ks[9], (3 * D_MODEL, D_MODEL), jnp.float32) * s, 'sa_out_w': jax.random.normal(ks[10], (D_MODEL, D_MODEL), jnp.float32) * s, 'q_w': jax.random.normal(ks[11], (D_MODEL, D_MODEL), jnp.float32) * s, 'k_w': jax.random.normal(ks[12], (D_MODEL, D_MODEL), jnp.float32) * s, 'v_w': jax.random.normal(ks[13], (D_MODEL, D_MODEL), jnp.float32) * s, 'ca_out_w': jax.random.normal(ks[14], (D_MODEL, D_MODEL), jnp.float32) * s, 'ffn_w1': jax.random.normal(ks[15], (D_FF, D_MODEL), jnp.float32) * s, 'ffn_b1': jax.random.normal(ks[16], (D_FF,), jnp.float32) * s, 'ffn_w2': jax.random.normal(ks[17], (D_MODEL, D_FF), jnp.float32) * s, 'ffn_b2': jax.random.normal(ks[18], (D_MODEL,), jnp.float32) * s}
        return inp
    _L0_xcond_all = _L0_xcond_setup()
    _L0_xcond_in = {k: v for k, v in _L0_xcond_all.items() if k in ('ln1_w', 'ln1_b', 'ln2_w', 'ln2_b', 'ln3_w', 'ln3_b', 'qkv_w', 'sa_out_w', 'q_w', 'k_w', 'v_w', 'ca_out_w', 'ffn_w1', 'ffn_b1', 'ffn_w2', 'ffn_b2')}
    del _L0_xcond_all
    return {'x': x, 'cond_1024': cond_1024, 'ctx_1024': ctx_1024, 'L0_xcond_ln1_w': _L0_xcond_in['ln1_w'], 'L0_xcond_ln1_b': _L0_xcond_in['ln1_b'], 'L0_xcond_ln2_w': _L0_xcond_in['ln2_w'], 'L0_xcond_ln2_b': _L0_xcond_in['ln2_b'], 'L0_xcond_ln3_w': _L0_xcond_in['ln3_w'], 'L0_xcond_ln3_b': _L0_xcond_in['ln3_b'], 'L0_xcond_qkv_w': _L0_xcond_in['qkv_w'], 'L0_xcond_sa_out_w': _L0_xcond_in['sa_out_w'], 'L0_xcond_q_w': _L0_xcond_in['q_w'], 'L0_xcond_k_w': _L0_xcond_in['k_w'], 'L0_xcond_v_w': _L0_xcond_in['v_w'], 'L0_xcond_ca_out_w': _L0_xcond_in['ca_out_w'], 'L0_xcond_ffn_w1': _L0_xcond_in['ffn_w1'], 'L0_xcond_ffn_b1': _L0_xcond_in['ffn_b1'], 'L0_xcond_ffn_w2': _L0_xcond_in['ffn_w2'], 'L0_xcond_ffn_b2': _L0_xcond_in['ffn_b2']}

def reference(x, cond_1024, ctx_1024, L0_xcond_ln1_w, L0_xcond_ln1_b, L0_xcond_ln2_w, L0_xcond_ln2_b, L0_xcond_ln3_w, L0_xcond_ln3_b, L0_xcond_qkv_w, L0_xcond_sa_out_w, L0_xcond_q_w, L0_xcond_k_w, L0_xcond_v_w, L0_xcond_ca_out_w, L0_xcond_ffn_w1, L0_xcond_ffn_b1, L0_xcond_ffn_w2, L0_xcond_ffn_b2):
    import jax
    import jax.numpy as jnp

    def _L0_xcond_ref(x, noise_emb, context, ln1_w, ln1_b, ln2_w, ln2_b, ln3_w, ln3_b, qkv_w, sa_out_w, q_w, k_w, v_w, ca_out_w, ffn_w1, ffn_b1, ffn_w2, ffn_b2):
        import jax, jax.numpy as jnp
        import numpy as np
        import math
        D_MODEL = 512
        N_HEADS = 16
        HEAD_DIM = D_MODEL // N_HEADS
        D_FF = 2048
        EPS = 1e-05
        ROPE_BASE = 10000.0

        def _rope(t):
            L, Dh = (t.shape[1], t.shape[-1])
            half = Dh // 2
            inv_freq = 1.0 / ROPE_BASE ** (jnp.arange(half, dtype=t.dtype) / half)
            ang = jnp.arange(L, dtype=t.dtype)[:, None] * inv_freq[None, :]
            cos = jnp.cos(ang)[None, :, None, :]
            sin = jnp.sin(ang)[None, :, None, :]
            t1, t2 = (t[..., :half], t[..., half:])
            return jnp.concatenate([t1 * cos - t2 * sin, t2 * cos + t1 * sin], axis=-1)

        def _adaln(x, emb, w, b):
            e = emb[:, 0, :]
            gb = e @ w.T + b
            gamma, beta = jnp.split(gb, 2, axis=-1)
            mu = x.mean(-1, keepdims=True)
            var = x.var(-1, keepdims=True)
            xn = (x - mu) * jax.lax.rsqrt(var + EPS)
            return xn * (1.0 + gamma[:, None, :]) + beta[:, None, :]

        def _attn(q, k, v):
            scale = 1.0 / math.sqrt(HEAD_DIM)
            scores = jnp.einsum('bqhd,bkhd->bhqk', q, k) * scale
            w = jax.nn.softmax(scores, axis=-1)
            out = jnp.einsum('bhqk,bkhd->bqhd', w, v)
            B, Lq = (out.shape[0], out.shape[1])
            return out.reshape(B, Lq, D_MODEL)
        B, L, D = x.shape
        L_ctx = context.shape[1]
        res = x
        xn = _adaln(x, noise_emb, ln1_w, ln1_b)
        qkv = xn @ qkv_w.T
        q, k, v = jnp.split(qkv, 3, axis=-1)
        q = _rope(q.reshape(B, L, N_HEADS, HEAD_DIM))
        k = _rope(k.reshape(B, L, N_HEADS, HEAD_DIM))
        v = v.reshape(B, L, N_HEADS, HEAD_DIM)
        sa = _attn(q, k, v) @ sa_out_w.T
        x = res + sa
        res = x
        xn = _adaln(x, noise_emb, ln2_w, ln2_b)
        q = _rope((xn @ q_w.T).reshape(B, L, N_HEADS, HEAD_DIM))
        k = _rope((context @ k_w.T).reshape(B, L_ctx, N_HEADS, HEAD_DIM))
        v = (context @ v_w.T).reshape(B, L_ctx, N_HEADS, HEAD_DIM)
        ca = _attn(q, k, v) @ ca_out_w.T
        x = res + ca
        res = x
        xn = _adaln(x, noise_emb, ln3_w, ln3_b)
        h = jax.nn.gelu(xn @ ffn_w1.T + ffn_b1, approximate=False)
        x = res + (h @ ffn_w2.T + ffn_b2)
        return x
    x = _L0_xcond_ref(x, cond_1024[:, None, :], ctx_1024, L0_xcond_ln1_w, L0_xcond_ln1_b, L0_xcond_ln2_w, L0_xcond_ln2_b, L0_xcond_ln3_w, L0_xcond_ln3_b, L0_xcond_qkv_w, L0_xcond_sa_out_w, L0_xcond_q_w, L0_xcond_k_w, L0_xcond_v_w, L0_xcond_ca_out_w, L0_xcond_ffn_w1, L0_xcond_ffn_b1, L0_xcond_ffn_w2, L0_xcond_ffn_b2)
    return x

_drawn_inputs = setup_inputs


def setup_inputs(seed=0):
    import zlib

    import numpy as np

    out = dict(_drawn_inputs(seed))
    spreads = {}
    factors = {'L0_xcond_ln1_b': 8.0,
     'L0_xcond_ln2_w': 8.0,
     'L0_xcond_ln2_b': 8.0,
     'L0_xcond_ln3_b': 8.0,
     'L0_xcond_q_w': 5.508,
     'L0_xcond_k_w': 6.488,
     'L0_xcond_ffn_b1': 5.651,
     'L0_xcond_ffn_b2': 3.144}
    for name, (base, spread) in spreads.items():
        noise = np.random.default_rng([zlib.crc32(name.encode()), seed]).standard_normal(out[name].shape)
        drawn = base * np.exp(spread * noise) if base else spread * noise
        out[name] = jnp.asarray(drawn.astype(out[name].dtype))
    for name, factor in factors.items():
        out[name] = (out[name] * factor).astype(out[name].dtype)
    return out
```

```python
from contextlib import ExitStack

import concourse.bass as bass
import numpy as np
from concourse import mybir

F32 = mybir.dt.float32
F32R = mybir.dt.float32r
ACT = mybir.ActivationFunctionType
ALU = mybir.AluOpType
AX = mybir.AxisListType

P = 128
EPS = 1e-5
ROPE_BASE = 10000.0


class Queue:

    def __init__(self, sem):
        self.sem, self.count, self.items = sem, 0, []

    def put(self, make, *tickets, signal=True):
        self.items.append((tickets, make, self.sem if signal else None, 1))
        self.count += 1 if signal else 0
        return (self.sem, self.count) if signal else None

    def dma(self, make, slot, *tickets):
        slot.count += 16
        self.items.append((tickets, make, slot.sem, 16))
        return (slot.sem, slot.count)

    def wait(self, *tickets):
        self.items.append((tickets, None, None, 0))

    def play(self, eng):
        reached = {}
        for tickets, make, sem, step in self.items:
            for ticket in tickets:
                if ticket is not None and reached.get(id(ticket[0]), 0) < ticket[1]:
                    eng.wait_ge(ticket[0], ticket[1])
                    reached[id(ticket[0])] = ticket[1]
            if make is not None:
                ins = make(eng)
                if sem is not None:
                    ins.then_inc(sem, step)


class Slot:

    def __init__(self, sem):
        self.sem, self.count = sem, 0


def block_kernel(nc, x, condT, ctxT, lnT, lnb, attnT, w1T, b1, w2T, b2, cos, sin, pick, ident_in, x1, x2, out):
    B, L, D = x.shape
    HALF = cos.shape[1]
    HD = 2 * HALF
    H = D // HD
    F = b1.shape[1] * P
    KC = D // P
    T = L // P
    HG = H // 2
    FC = F // P
    SCALE = float(HD) ** -0.5
    ROWS = 3 * HD
    MROWS = ROWS + 2 * HG
    VW = HD + 1
    OH = 4
    N_ITEMS = 2 * B

    with ExitStack() as whole:
        def sem(name):
            return whole.enter_context(nc.semaphore(name))

        def keep(name, shape, dt=F32):
            return whole.enter_context(nc.sbuf_tensor(name, shape, dt))

        ident = keep("ident", [P, P])
        gb = keep("gb", [P, 3, 2 * KC, B])
        neg_half = keep("neg_half", [P, T])
        pe, act, dve, pool, sp = (Queue(sem(n)) for n in ("pe_done", "act_done", "dve_done", "pool_done", "sp_done"))
        slots = {}

        def slot(name):
            if name not in slots:
                slots[name] = Slot(sem(name))
            return slots[name]

        def run(queues):
            with nc.Block() as block:
                @block.tensor
                def _(eng):
                    pe.play(eng)

                @block.scalar
                def _(eng):
                    act.play(eng)

                @block.vector
                def _(eng):
                    dve.play(eng)

                @block.gpsimd
                def _(eng):
                    pool.play(eng)

                @block.sync
                def _(eng):
                    sp.play(eng)
            for q in queues:
                q.items = []

        queues = (pe, act, dve, pool, sp)

        with ExitStack() as stage:
            def sb(name, shape, dt=F32):
                return stage.enter_context(nc.sbuf_tensor(name, shape, dt))

            ln_w = sb("ln_w", [P, 3, KC, 2 * D])
            cond_sb = sb("cond_sb", [P, KC, B])
            ln_b = sb("ln_b", [P, 3, 2 * KC])
            ps = stage.enter_context(nc.psum_tensor("mod_ps", [P, 3, 512], F32))
            small = [sp.dma(lambda e: e.dma_start(cond_sb[:, :, :], condT.rearrange("(c p) b -> p c b", p=P)), slot("cond_in")),
                     sp.dma(lambda e: e.dma_start(ln_b[:, :, :], lnb), slot("lnb_in")),
                     sp.dma(lambda e: e.dma_start(ident[:, :], ident_in), slot("ident_in"))]
            dve.put(lambda e: e.memset(neg_half[:, :], -0.5))
            for n in range(3):
                w_in = sp.dma(lambda e, n=n: e.dma_start(ln_w[:, n, :, :], lnT[n].rearrange("(c p) o -> p c o", p=P)), slot(f"lnw_in{n}"))
                for m in range(2 * KC):
                    for c in range(KC):
                        got = pe.put(lambda e, n=n, m=m, c=c: e.matmul(
                            ps[:, n, m * B:(m + 1) * B], ln_w[:, n, c, m * P:(m + 1) * P], cond_sb[:, c, :],
                            start=c == 0, stop=c == KC - 1), w_in, *small, signal=m == 2 * KC - 1 and c == KC - 1)
                added = dve.put(lambda e, n=n: e.tensor_tensor(
                    gb[:, n, :, :], ps[:, n, 0:2 * KC * B].rearrange("p (m b) -> p m b", b=B),
                    ln_b[:, n, :].unsqueeze(2).broadcast_to([P, 2 * KC, B]), ALU.add), got, small[1])
                gb_ready = dve.put(lambda e, n=n: e.tensor_scalar(
                    gb[:, n, 0:KC, :], gb[:, n, 0:KC, :], 1.0, None, ALU.add), added)
            run(queues)

        with ExitStack() as stage:
            def sb(name, shape, dt=F32):
                return stage.enter_context(nc.sbuf_tensor(name, shape, dt))

            MATS = ("q", "k", "v", "o")
            w_hi = {m: sb(f"w_hi_{m}", [P, KC, D], F32R) for m in MATS}
            w_lo = {m: sb(f"w_lo_{m}", [P, KC, D], F32R) for m in MATS}
            w_raw = [sb(f"w_raw{i}", [P, D]) for i in range(2)]
            cos_sb = sb("cos_sb", [P, T, HALF])
            pick_sb = sb("pick_sb", [P, HG])
            sin_sb = sb("sin_sb", [P, T, 2, HALF])
            xn = sb("xn", [P, T, D])
            res = sb("res", [P, T, D])
            stats = sb("stats", [P, T, 6])
            mv = sb("mv", [P, T, 2])
            rstd_in = sb("rstd_in", [P, T])
            rstd = sb("rstd", [P, T])
            xT = sb("xT", [P, KC, L])
            x_hi = sb("x_hi", [P, KC, L], F32R)
            x_lo = sb("x_lo", [P, KC, L], F32R)
            ctx_hi = sb("ctx_hi", [P, KC, L], F32R)
            ctx_lo = sb("ctx_lo", [P, KC, L], F32R)
            rope_c = [sb(f"rope_c{i}", [P, D]) for i in range(2)]
            rope_s = sb("rope_s", [P, D])
            stack = {m: sb(f"stack_{m}", [P, T, H, 3, HD], F32R) for m in "qk"}
            NG = 3
            qT = sb("qT", [MROWS, NG, HG, L], F32R)
            kT = sb("kT", [MROWS, NG, HG, L], F32R)
            NV = 2
            v_sb = [sb(f"v_sb{i}", [P, T, H, VW]) for i in range(NV)]
            neg_max = sb("neg_max", [P, T, HG])
            max_parts = sb("max_parts", [P, T, 2, HG])
            maxT = sb("maxT", [2 * HG, L], F32R)
            NP = 3
            prob = sb("prob", [P, NP, T, L])
            rden = sb("rden", [P, OH, T])
            o_sb = sb("o_sb", [P, T, D])
            o_hi = sb("o_hi", [P, KC, L], F32R)
            o_lo = sb("o_lo", [P, KC, L], F32R)

            def psum(name, n):
                return stage.enter_context(nc.psum_tensor(name, [P, n, 512], F32))

            ps_s = psum("ps_s", 2)
            ps_t = psum("ps_t", 2)
            ps_o = psum("ps_o", 1)
            NB = 3
            ps_g = psum("ps_g", NB)

            tables = [sp.dma(lambda e: e.dma_start(cos_sb[:, :, :], cos.rearrange("(t p) d -> p t d", p=P)), slot("cos_in")),
                      sp.dma(lambda e: e.dma_start(sin_sb[:, :, :, :], sin.rearrange("(t p) s d -> p t s d", p=P)), slot("sin_in"))]
            tables.append(sp.dma(lambda e: e.dma_start(pick_sb[ROWS:MROWS, :], pick), slot("pick_in")))
            ones = [dve.put(lambda e, r=r: e.tensor_copy(
                kT[ROWS:MROWS, r, :, :], pick_sb[ROWS:MROWS, :].unsqueeze(2).broadcast_to([2 * HG, HG, L])), tables[-1])
                for r in range(NG)]
            ones += [dve.put(lambda e, i=i: e.memset(v_sb[i][:, :, :, HD:VW], 1.0)) for i in range(NV)]

            bank_reader = [None] * NB
            bank_turn = [0]

            def take_bank():
                n = bank_turn[0] % NB
                bank_turn[0] += 1
                return n, bank_reader[n]

            w_ready = {}
            w_last_use = {m: None for m in MATS}
            raw_free = [None, None]

            def load_weight(layer, m):
                n = MATS.index(m)
                for c in range(KC):
                    r = c % 2
                    loaded = sp.dma(lambda e, c=c, r=r: e.dma_start(w_raw[r][:, :], attnT[layer, n, c * P:(c + 1) * P, :]),
                                    slot(f"w_raw_in{r}"), raw_free[r])
                    hi = act.put(lambda e, c=c, r=r: e.activation(w_hi[m][:, c, :], w_raw[r][:, :], ACT.Copy),
                                 loaded, w_last_use[m])
                    lo = dve.put(lambda e, c=c, r=r: e.tensor_tensor(
                        w_lo[m][:, c, :], w_raw[r][:, :], w_hi[m][:, c, :].bitcast(F32), ALU.subtract), hi)
                    raw_free[r] = lo
                w_ready[m] = lo

            last = {name: None for name in ("xn_read", "xT", "x_split", "ctx_split", "stack_q", "stack_k", "o_sb", "o_split")}
            x_loaded, res_loaded, stored = {}, {}, {}

            def load_x(i):
                layer, b = divmod(i, B)
                src = x if layer == 0 else x1
                x_loaded[i] = sp.dma(lambda e: e.dma_start(xn[:, :, :], src[b].rearrange("(t p) d -> p t d", p=P)),
                                     slot("x_in"), last["xn_read"], stored.get((layer - 1, b)))

            def load_res(i):
                layer, b = divmod(i, B)
                src = x if layer == 0 else x1
                res_loaded[i] = sp.dma(lambda e: e.dma_start(res[:, :, :], src[b].rearrange("(t p) d -> p t d", p=P)),
                                       slot("res_in"), stored.get(divmod(i - 1, B)), stored.get((layer - 1, b)))

            rope_free = [None, None]
            group_ready = {}
            group_done = {}
            v_ready, v_done = {}, {}
            rope_turn = [0]

            def norm(i):
                layer, b = divmod(i, B)
                for t in range(T):
                    dve.put(lambda e, t=t: e.bn_stats(stats[:, t, :], xn[:, t, :]), x_loaded[i])
                s = (dve.sem, dve.count)
                for t in range(T):
                    a = dve.put(lambda e, t=t: e.bn_aggr(mv[:, t, :], stats[:, t, :]), s)
                shifted = dve.put(lambda e: e.tensor_scalar(rstd_in[:, :], mv[:, :, 1], EPS, None, ALU.add), a)
                root = pool.put(lambda e: e.tensor_tensor(rstd[:, :], rstd_in[:, :], neg_half[:, :], ALU.pow), shifted)
                for t in range(T):
                    last["xn"] = dve.put(lambda e, t=t: e.tensor_scalar(
                        xn[:, t, :], xn[:, t, :], mv[:, t, 0:1], rstd[:, t:t + 1], ALU.subtract, ALU.mult), root)

            def transpose_x(i, half):
                layer, b = divmod(i, B)
                n, free = take_bank()
                for c in range(2):
                    for t in range(T):
                        k = 2 * half + c
                        done = pe.put(lambda e, c=c, t=t, k=k: e.transpose(
                            ps_g[:, n, c * L + t * P:c * L + (t + 1) * P], xn[:, t, k * P:(k + 1) * P], ident[:, :]),
                            last["xn"], free)
                last["xn_read"] = done
                for c in range(2):
                    k = 2 * half + c
                    full = act.put(lambda e, c=c, k=k: e.activation(
                        xT[:, k, :], ps_g[:, n, c * L:(c + 1) * L], ACT.Identity,
                        bias=gb[:, layer, KC + k, b:b + 1], scale=gb[:, layer, k, b:b + 1]), done, last["xT"])
                bank_reader[n] = full
                ks = slice(2 * half, 2 * half + 2)
                hi = act.put(lambda e: e.activation(x_hi[:, ks, :], xT[:, ks, :], ACT.Copy), full, last["x_split"])
                lo = dve.put(lambda e: e.tensor_tensor(x_lo[:, ks, :], xT[:, ks, :], x_hi[:, ks, :].bitcast(F32), ALU.subtract), hi)
                last["xT_next"] = lo
                return lo

            def split_ctx(i):
                b = i % B
                full = sp.dma(lambda e: e.dma_start(xT[:, :, :], ctxT[b].rearrange("(c p) l -> p c l", p=P)), slot("ctx_in"), last["xT"])
                hi = act.put(lambda e: e.activation(ctx_hi[:, :, :], xT[:, :, :], ACT.Copy), full, last["ctx_split"])
                lo = dve.put(lambda e: e.tensor_tensor(ctx_lo[:, :, :], xT[:, :, :], ctx_hi[:, :, :].bitcast(F32), ALU.subtract), hi)
                last["xT"] = lo
                return lo

            def project(m, t, hi, lo, ready):
                n, free = take_bank()
                steps = [(a, w, c) for c in range(KC) for a, w in ((hi, w_hi), (hi, w_lo), (lo, w_hi))]
                for j, (a, w, c) in enumerate(steps):
                    done = pe.put(lambda e, a=a, w=w, c=c, j=j: e.matmul(
                        ps_g[:, n, :], a[:, c, t * P:(t + 1) * P], w[m][:, c, :], start=j == 0, stop=j == len(steps) - 1),
                        ready, w_ready[m], free, signal=j == len(steps) - 1)
                w_last_use[m] = done
                return n, done

            def rope_and_stack(m, t, n, done):
                r = rope_turn[0] % 2
                rope_turn[0] += 1
                c_out, s_out = rope_c[r], rope_s
                src = ps_g[:, n, :].rearrange("p (h s d) -> p h s d", s=2, d=HALF)
                dst = c_out[:, :].rearrange("p (h d) -> p h d", d=HALF)
                c_done = dve.put(lambda e: e.tensor_tensor(
                    dst, ps_g[:, n, :].rearrange("p (h d) -> p h d", d=HALF),
                    cos_sb[:, t, :].unsqueeze(1).broadcast_to([P, 2 * H, HALF]), ALU.mult), done, rope_free[r], *tables)
                s_done = dve.put(lambda e: e.tensor_tensor(
                    s_out[:, :].rearrange("p (h s d) -> p h s d", s=2, d=HALF), src[:, :, ::-1, :],
                    sin_sb[:, t, :, :].unsqueeze(1).broadcast_to([P, H, 2, HALF]), ALU.mult), last.get("rope_s"))
                bank_reader[n] = s_done
                total = pool.put(lambda e: e.tensor_tensor(c_out[:, :], c_out[:, :], s_out[:, :], ALU.add), s_done)
                last["rope_s"] = total
                st = stack[m][:, t, :, :, :]
                whole_head = c_out[:, :].rearrange("p (h d) -> p h d", d=HD)
                two = slice(0, 2) if m == "q" else slice(0, 3, 2)
                one = 2 if m == "q" else 1
                hi = act.put(lambda e: e.activation(st[:, :, two, :], whole_head.unsqueeze(2).broadcast_to([P, H, 2, HD]),
                                                    ACT.Copy), total, last[f"stack_{m}"])
                lo = dve.put(lambda e: e.tensor_tensor(st[:, :, one, :], whole_head, st[:, :, 0, :].bitcast(F32),
                                                       ALU.subtract), hi, last[f"stack_{m}"])
                rope_free[r] = lo
                return lo

            def spread(i, m, g, t, half, ready):
                n, free = take_bank()
                ring = (2 * i + g) % NG
                dst = qT if m == "q" else kT
                prev = group_done.get((2 * i + g - NG))
                for j in range(4):
                    h = g * HG + half * 4 + j
                    done = pe.put(lambda e, j=j, h=h: e.transpose(
                        ps_g[0:ROWS, n, j * P:(j + 1) * P],
                        stack[m][:, t, h, :, :].rearrange("p s d -> p (s d)").bitcast(F32), ident[:, :]),
                        ready, free, signal=j == 3)
                last[f"stack_{m}_next"] = done
                out_ap = dst[0:ROWS, ring, half * 4:half * 4 + 4, t * P:(t + 1) * P]
                in_ap = ps_g[0:ROWS, n, :].rearrange("p (h l) -> p h l", l=P)
                copied = act.put(lambda e: e.activation(out_ap, in_ap, ACT.Copy), done, prev)
                bank_reader[n] = copied
                group_ready.setdefault((i, g), []).append(copied)

            def prepare(i):
                layer, b = divmod(i, B)
                s = {}

                def first():
                    norm(i)
                    if layer:
                        s["ctx"] = split_ctx(i)
                yield 0.0, first
                if layer:
                    kv_hi, kv_lo = ctx_hi, ctx_lo
                else:
                    kv_hi, kv_lo = x_hi, x_lo

                def turn_x():
                    transpose_x(i, 0)
                    s["x"] = transpose_x(i, 1)
                    if i + 1 < N_ITEMS:
                        load_x(i + 1)
                    last["xT"] = last["xT_next"]
                    if not layer:
                        s["ctx"] = s["x"]

                def qk(m, t):
                    def piece():
                        if m == "k":
                            n, done = project("k", t, kv_hi, kv_lo, s["ctx"])
                        else:
                            n, done = project("q", t, x_hi, x_lo, s["x"])
                        s["last_" + m] = done
                        s[m, t] = rope_and_stack(m, t, n, done)
                    return piece

                def v(t):
                    def piece():
                        n, done = project("v", t, kv_hi, kv_lo, s["ctx"])
                        dst = v_sb[i % NV]
                        v_ready[i] = act.put(lambda e: e.activation(
                            dst[:, t, :, 0:HD], ps_g[:, n, :].rearrange("p (h d) -> p h d", d=HD), ACT.Copy),
                            done, v_done.get(i - NV))
                        bank_reader[n] = v_ready[i]
                        if t == T - 1:
                            last["x_split"] = done
                            last["ctx_split"] = done
                            if i % B == B - 1 and layer == 0:
                                for m in ("k", "v", "q"):
                                    load_weight(1, m)
                    return piece

                def turn(m, g, t, half):
                    def piece():
                        spread(i, m, g, t, half, s[m, t])
                        if (g, t, half) == (1, T - 1, 1):
                            last[f"stack_{m}"] = last[f"stack_{m}_next"]
                    return piece

                gemm = 12 * 0.216
                if layer:
                    order = [("k", 0), ("k", 1), ("x",), ("q", 0), ("q", 1), ("v", 0), ("v", 1)]
                else:
                    order = [("x",), ("k", 0), ("k", 1), ("q", 0), ("q", 1), ("v", 0), ("v", 1)]
                turns = []
                for o in order:
                    if o[0] == "x":
                        yield 0.9, turn_x
                    elif o[0] == "v":
                        yield "early", gemm, v(o[1])
                    else:
                        yield gemm, qk(*o)
                for g in range(2):
                    for m in "kq":
                        for t in range(T):
                            for half in range(2):
                                yield ("early", "late")[g], 0.25, turn(m, g, t, half)

            GEMM_COST = 12 * 0.216
            FINISH_COST = 2 * 0.25 + T * GEMM_COST

            score_reader = [None, None]
            probT_reader = [None, None]
            prob_reader = [None] * NP
            out_reader = [None]
            max_ready = {}
            slot_turn = {"s": 0, "t": 0}

            def scores(G, j):
                i, g = divmod(G, 2)
                n = slot_turn["s"] % 2
                slot_turn["s"] += 1
                ring = G % NG
                for t in range(T):
                    done = pe.put(lambda e, t=t: e.matmul(
                        ps_s[:, n, t * L:(t + 1) * L], qT[0:ROWS, ring, j, t * P:(t + 1) * P], kT[0:ROWS, ring, j, :],
                        start=True, stop=True), *group_ready[i, g], score_reader[n], signal=t == T - 1)
                score_reader[n] = dve.put(lambda e: e.tensor_reduce(
                    neg_max[:, :, j], ps_s[:, n, :].rearrange("p (t l) -> p t l", l=L), AX.X, ALU.max, negate=True),
                    done, last.get("neg_max"))

            def spread_max(G):
                ring = G % NG
                hi = dve.put(lambda e: e.tensor_copy(max_parts[:, :, 0, :].bitcast(F32R), neg_max[:, :, :]),
                             score_reader[0], score_reader[1], last.get("max_parts"))
                lo = dve.put(lambda e: e.tensor_tensor(max_parts[:, :, 1, :], neg_max[:, :, :], max_parts[:, :, 0, :],
                                                       ALU.subtract), hi)
                last["neg_max"] = lo
                n, free = take_bank()
                for t in range(T):
                    done = pe.put(lambda e, t=t: e.transpose(
                        ps_g[0:2 * HG, n, t * P:(t + 1) * P], max_parts[:, t, :, :].rearrange("p s h -> p (s h)"), ident[:, :]),
                        lo, free, signal=t == T - 1)
                last["max_parts"] = done
                copied = act.put(lambda e: e.activation(maxT[:, :], ps_g[0:2 * HG, n, 0:L], ACT.Copy), done, *last.get("maxT", ()))
                bank_reader[n] = copied
                moved = [sp.dma(lambda e: e.dma_start(
                    qT[ROWS:MROWS, ring, :, :].bitcast(F32), maxT[:, :].bitcast(F32).unsqueeze(1).broadcast_to([2 * HG, HG, L])),
                    slot("max_in"), copied)]
                last["maxT"] = moved
                max_ready[G] = moved

            def weigh(G, j):
                i, g = divmod(G, 2)
                n = slot_turn["t"] % 2
                p = slot_turn["t"] % NP
                slot_turn["t"] += 1
                ring = G % NG
                for t in range(T):
                    done = pe.put(lambda e, t=t: e.matmul(
                        ps_t[:, n, t * L:(t + 1) * L], kT[:, ring, j, t * P:(t + 1) * P], qT[:, ring, j, :],
                        start=True, stop=True), *max_ready[G], *ones, probT_reader[n], signal=t == T - 1)
                group_done[G] = done
                weighed = act.put(lambda e: e.activation(
                    prob[:, p, :, :].rearrange("p t l -> p (t l)"), ps_t[:, n, :], ACT.Exp, scale=SCALE),
                    done, prob_reader[p])
                probT_reader[n] = weighed
                return p, weighed

            def mix(G, j, p, weighed):
                i, g = divmod(G, 2)
                h = g * HG + j
                o = j % OH
                base = o * T * VW
                for t in range(T):
                    for k in range(T):
                        done = pe.put(lambda e, t=t, k=k: e.matmul(
                            ps_o[:, 0, base + t * VW:base + (t + 1) * VW], prob[:, p, k, t * P:(t + 1) * P],
                            v_sb[i % NV][:, k, h, :], start=k == 0, stop=k == T - 1),
                            weighed, v_ready[i], *ones, out_reader[0] if o == 0 else None, signal=(t, k) == (T - 1, T - 1))
                prob_reader[p] = done
                if h == H - 1:
                    v_done[i] = done
                if o == OH - 1:
                    got = ps_o[:, 0, 0:OH * T * VW].rearrange("p (h t w) -> p h t w", t=T, w=VW)
                    inv = dve.put(lambda e: e.reciprocal(rden[:, :, :], got[:, :, :, HD]), done, out_reader[0])
                    for t in range(T):
                        last["o_sb"] = dve.put(lambda e, t=t: e.tensor_tensor(
                            o_sb[:, t, (h - OH + 1) * HD:(h + 1) * HD].rearrange("p (h d) -> p h d", d=HD),
                            got[:, :, t, 0:HD], rden[:, :, t].unsqueeze(2).broadcast_to([P, OH, HD]), ALU.mult),
                            inv, last.get("o_read"))
                    out_reader[0] = last["o_sb"]

            def finish(i):
                layer, b = divmod(i, B)
                s = {}

                def turn_o(half):
                    def piece():
                        n, free = take_bank()
                        for c in range(2):
                            k = 2 * half + c
                            for t in range(T):
                                done = pe.put(lambda e, c=c, t=t, k=k: e.transpose(
                                    ps_g[:, n, c * L + t * P:c * L + (t + 1) * P], o_sb[:, t, k * P:(k + 1) * P], ident[:, :]),
                                    s["o"], free, signal=(c, t) == (1, T - 1))
                        ks = slice(2 * half, 2 * half + 2)
                        got = ps_g[:, n, :].rearrange("p (c l) -> p c l", l=L)
                        hi = act.put(lambda e: e.activation(o_hi[:, ks, :], got, ACT.Copy), done, last["o_split"])
                        s["split"] = dve.put(lambda e: e.tensor_tensor(
                            o_lo[:, ks, :], got, o_hi[:, ks, :].bitcast(F32), ALU.subtract), hi)
                        bank_reader[n] = s["split"]
                        if half == 1:
                            last["o_read"] = done
                    return piece

                def out_proj(t):
                    def piece():
                        n, done = project("o", t, o_hi, o_lo, s["split"])
                        added = dve.put(lambda e: e.tensor_tensor(res[:, t, :], ps_g[:, n, :], res[:, t, :], ALU.add),
                                        done, res_loaded[i])
                        bank_reader[n] = added
                        if t == T - 1:
                            last["o_split"] = done
                            dst = x1 if layer == 0 else x2
                            stored[layer, b] = sp.dma(lambda e: e.dma_start(
                                dst[b].rearrange("(t p) d -> p t d", p=P), res[:, :, :]), slot("x_out"), added)
                            if i == B - 1:
                                load_weight(1, "o")
                    return piece

                def start():
                    s["o"] = last["o_sb"]
                    load_res(i)
                start()
                yield 0.25, turn_o(0)
                yield 0.25, turn_o(1)
                for t in range(T):
                    yield 12 * 0.216, out_proj(t)

            load_x(0)
            for m in ("k", "q", "v", "o"):
                load_weight(0, m)
            late = []
            for *kind, _, piece in prepare(0):
                if kind == ["late"]:
                    late.append((0.25, piece))
                else:
                    piece()
            fill = []
            behind = None
            for G in range(2 * N_ITEMS + 1):
                i, g = divmod(G, 2)
                held = []
                if g == 0:
                    fill, late = late, []
                    if i + 1 < N_ITEMS:
                        for *kind, cost, piece in prepare(i + 1):
                            (late if kind == ["late"] else held if kind else fill).append((cost, piece))
                        budget = (sum(c for c, _ in fill + held) + FINISH_COST) / 2
                    else:
                        budget = 1e9
                    next_early = held
                elif i >= 1:
                    fill = list(finish(i - 1)) + fill + next_early
                    budget = 1e9
                else:
                    fill = fill + next_early
                    budget = 1e9
                total = min(budget, sum(c for c, _ in fill))
                spent = 0.0
                for j in range(HG):
                    if G < 2 * N_ITEMS:
                        scores(G, j)
                    if G >= 1:
                        now = (G - 1, j, *weigh(G - 1, j))
                        if behind:
                            mix(*behind)
                        behind = now
                    goal = total * (j + 1) / HG
                    while fill and (spent + fill[0][0] / 2 <= goal or (budget == 1e9 and j == HG - 1)):
                        cost, piece = fill.pop(0)
                        piece()
                        spent += cost
                if behind:
                    mix(*behind)
                    behind = None
                if G < 2 * N_ITEMS:
                    spread_max(G)
            for _, piece in fill:
                piece()
            for _, piece in finish(N_ITEMS - 1):
                piece()
            run(queues)

        with ExitStack() as stage:
            def sb(name, shape, dt=F32):
                return stage.enter_context(nc.sbuf_tensor(name, shape, dt))

            U = 4 * P
            UT = U // P
            NU = B * L // U
            w1_hi, w1_lo = (sb(f"w1_{s}", [P, FC, KC, P], F32R) for s in ("hi", "lo"))
            w2_hi, w2_lo = (sb(f"w2_{s}", [P, FC, D], F32R) for s in ("hi", "lo"))
            NR = 2
            raw = [sb(f"f_raw{i}", [P, 2 * D]) for i in range(NR)]
            b1_sb = sb("b1_sb", [P, FC])
            b2_sb = sb("b2_sb", [P, D])
            xn = sb("f_xn", [P, UT, D])
            res = sb("f_res", [P, UT, D])
            stats = sb("f_stats", [P, UT, 6])
            mv = sb("f_mv", [P, UT, 2])
            rstd_in = sb("f_rstd_in", [P, UT])
            rstd = sb("f_rstd", [P, UT])
            half_sb = sb("f_half", [P, UT])
            xT = sb("f_xT", [P, U])
            x_hi = [sb(f"f_x_hi{i}", [P, KC, U], F32R) for i in range(2)]
            x_lo = [sb(f"f_x_lo{i}", [P, KC, U], F32R) for i in range(2)]
            NH = 2
            h_sb = [sb(f"h_sb{i}", [P, U]) for i in range(2)]
            h_hi = [sb(f"h_hi{i}", [P, U], F32R) for i in range(NH)]
            h_lo = [sb(f"h_lo{i}", [P, U], F32R) for i in range(NH)]

            ps_y = stage.enter_context(nc.psum_tensor("ps_y", [P, UT, 512], F32))
            ps_h = stage.enter_context(nc.psum_tensor("ps_h", [P, 2, 512], F32))
            ps_x = stage.enter_context(nc.psum_tensor("ps_x", [P, 2, 512], F32))

            sp_b = [sp.dma(lambda e: e.dma_start(b1_sb[:, :], b1), slot("b1_in")),
                    sp.dma(lambda e: e.dma_start(b2_sb[:, :], b2.partition_broadcast(P)), slot("b2_in"))]
            half_set = dve.put(lambda e: e.memset(half_sb[:, :], -0.5))
            state = {"xn_read": None, "xT_read": None, "bank": [None, None], "turn": 0, "sent": ()}
            x_loaded, res_loaded = {}, {}

            def load(u, dst, name, *free):
                per = U // L
                return [sp.dma(lambda e, j=j: e.dma_start(
                    dst[:, j * T:(j + 1) * T, :], x2[u * per + j].rearrange("(t p) d -> p t d", p=P)),
                    slot(f"{name}{j}"), *free) for j in range(per)]

            x_loaded[0] = load(0, xn, "f_x_in")
            w1_ready, w2_ready, raw_free = {}, {}, [None] * NR
            turn = 0
            for c2 in range(FC // 2):
                for which in (1, 2):
                    r = turn % NR
                    turn += 1
                    fs = slice(2 * c2, 2 * c2 + 2)
                    if which == 1:
                        src = w1T[:, 2 * c2 * P:2 * (c2 + 1) * P].rearrange("(k p) f -> p k f", p=P)
                        dst = raw[r][:, :].rearrange("p (k f) -> p k f", k=KC)
                        view = raw[r][:, :].rearrange("p (k c f) -> p c k f", k=KC, f=P)
                        hi_ap, lo_ap = w1_hi[:, fs, :, :], w1_lo[:, fs, :, :]
                    else:
                        src = w2T[2 * c2 * P:2 * (c2 + 1) * P, :].rearrange("(c p) d -> p c d", p=P)
                        dst = raw[r][:, :].rearrange("p (c d) -> p c d", c=2)
                        view = dst
                        hi_ap, lo_ap = w2_hi[:, fs, :], w2_lo[:, fs, :]
                    loaded = sp.dma(lambda e, dst=dst, src=src: e.dma_start(dst, src), slot(f"f_raw_in{r}"), raw_free[r])
                    hi = act.put(lambda e, a=hi_ap, v=view: e.activation(a, v, ACT.Copy), loaded)
                    lo = dve.put(lambda e, a=lo_ap, v=view, h=hi_ap: e.tensor_tensor(a, v, h.bitcast(F32), ALU.subtract), hi)
                    raw_free[r] = lo
                    for c in range(2 * c2, 2 * c2 + 2):
                        (w1_ready if which == 1 else w2_ready)[c] = lo

            x_split_read = [None, None]
            x_ready, res_ready = {}, {}

            def norm_unit(u):
                for t in range(UT):
                    dve.put(lambda e, t=t: e.bn_stats(stats[:, t, :], xn[:, t, :]), *x_loaded[u])
                s = (dve.sem, dve.count)
                for t in range(UT):
                    a = dve.put(lambda e, t=t: e.bn_aggr(mv[:, t, :], stats[:, t, :]), s)
                shifted = dve.put(lambda e: e.tensor_scalar(rstd_in[:, :], mv[:, :, 1], EPS, None, ALU.add), a)
                root = pool.put(lambda e: e.tensor_tensor(rstd[:, :], rstd_in[:, :], half_sb[:, :], ALU.pow), shifted, half_set)
                for t in range(UT):
                    state["xn"] = dve.put(lambda e, t=t: e.tensor_scalar(
                        xn[:, t, :], xn[:, t, :], mv[:, t, 0:1], rstd[:, t:t + 1], ALU.subtract, ALU.mult), root)

            def residual(u):
                loaded = load(u, res, "f_res_in", *state["sent"])
                for t in range(UT):
                    res_ready[u] = pool.put(lambda e, t=t: e.tensor_tensor(res[:, t, :], res[:, t, :], b2_sb[:, :], ALU.add),
                                            *loaded, sp_b[1])

            def turn_unit(u, k):
                n = state["turn"] % 2
                state["turn"] += 1
                for t in range(UT):
                    done = pe.put(lambda e, t=t: e.transpose(
                        ps_x[:, n, t * P:(t + 1) * P], xn[:, t, k * P:(k + 1) * P], ident[:, :]),
                        state["xn"], state["bank"][n], signal=t == UT - 1)
                state["xn_read"] = done
                per = U // L
                for j in range(per):
                    b = u * per + j
                    full = act.put(lambda e, j=j, b=b: e.activation(
                        xT[:, j * L:(j + 1) * L], ps_x[:, n, j * L:(j + 1) * L], ACT.Identity,
                        bias=gb[:, 2, KC + k, b:b + 1], scale=gb[:, 2, k, b:b + 1]), done, state["xT_read"])
                state["bank"][n] = full
                hi = act.put(lambda e: e.activation(x_hi[u % 2][:, k, :], xT[:, :], ACT.Copy), full, x_split_read[u % 2])
                x_ready[u] = dve.put(lambda e: e.tensor_tensor(
                    x_lo[u % 2][:, k, :], xT[:, :], x_hi[u % 2][:, k, :].bitcast(F32), ALU.subtract), hi, x_split_read[u % 2])
                state["xT_read"] = x_ready[u]

            h_reader = [None] * NH
            ps_h_reader = [None, None]
            h_ready = {}
            hidden = [0]

            def up(u, c):
                a = hidden[0]
                hidden[0] += 1
                n, r, f = a % 2, a % NH, a % 2
                steps = [(w, xx, k) for k in range(KC) for w, xx in ((w1_hi, x_hi[u % 2]), (w1_lo, x_hi[u % 2]), (w1_hi, x_lo[u % 2]))]
                for j, (w, xx, k) in enumerate(steps):
                    done = pe.put(lambda e, w=w, xx=xx, k=k, j=j: e.matmul(
                        ps_h[:, n, :], w[:, c, k, :], xx[:, k, :], start=j == 0, stop=j == len(steps) - 1),
                        x_ready[u], w1_ready[c], ps_h_reader[n], signal=j == len(steps) - 1)
                if c == FC - 1:
                    x_split_read[u % 2] = done
                g = act.put(lambda e: e.activation(h_sb[f][:, :], ps_h[:, n, :], ACT.Gelu, bias=b1_sb[:, c:c + 1]),
                            done, sp_b[0], state.get(("h", f)))
                ps_h_reader[n] = g
                hi = act.put(lambda e: e.activation(h_hi[r][:, :], h_sb[f][:, :], ACT.Copy), g, h_reader[r])
                lo = dve.put(lambda e: e.tensor_tensor(h_lo[r][:, :], h_sb[f][:, :], h_hi[r][:, :].bitcast(F32), ALU.subtract),
                             hi, h_reader[r])
                state["h", f] = lo
                h_ready[u, c] = (r, lo)

            y_reader = [None] * UT

            def down(u, c):
                r, ready = h_ready[u, c]
                for t in range(UT):
                    for j, (a, w) in enumerate(((h_hi[r], w2_hi), (h_hi[r], w2_lo), (h_lo[r], w2_hi))):
                        done = pe.put(lambda e, t=t, a=a, w=w, j=j: e.matmul(
                            ps_y[:, t, :], a[:, t * P:(t + 1) * P], w[:, c, :],
                            start=c == 0 and j == 0, stop=c == FC - 1 and j == 2),
                            ready, w2_ready[c], y_reader[t] if c == 0 else None, signal=j == 2)
                    if c == FC - 1:
                        y_reader[t] = dve.put(lambda e, t=t: e.tensor_tensor(res[:, t, :], ps_y[:, t, :], res[:, t, :], ALU.add),
                                              done, res_ready[u])
                h_reader[r] = done
                if c == FC - 1:
                    per = U // L
                    state["sent"] = [sp.dma(lambda e, j=j: e.dma_start(
                        out[u * per + j].rearrange("(t p) d -> p t d", p=P), res[:, j * T:(j + 1) * T, :]),
                        slot(f"f_x_out{j}"), y_reader[(j + 1) * T - 1]) for j in range(per)]
                    if u + 1 < NU:
                        residual(u + 1)
                    else:
                        sp.wait(*state["sent"])

            norm_unit(0)
            residual(0)
            for k in range(KC):
                turn_unit(0, k)
            x_loaded[1] = load(1, xn, "f_x_in", state["xn_read"])
            LAG = 1
            chunks = [(u, c) for u in range(NU) for c in range(FC)]
            for n in range(len(chunks) + LAG):
                if n < len(chunks):
                    u, c = chunks[n]
                    up(u, c)
                    if u + 1 < NU:
                        if c == FC - KC - 4:
                            norm_unit(u + 1)
                        if FC - KC - 1 <= c < FC - 1:
                            turn_unit(u + 1, c - (FC - KC - 1))
                        if c == FC - 1 and u + 2 < NU:
                            x_loaded[u + 2] = load(u + 2, xn, "f_x_in", state["xn_read"])
                if n >= LAG:
                    down(*chunks[n - LAG])
            run(queues)


def rope_tables(length, half):
    inv_freq = (1.0 / np.float32(ROPE_BASE) ** (np.arange(half, dtype=np.float32) / np.float32(half))).astype(np.float32)
    ang = np.arange(length, dtype=np.float32)[:, None] * inv_freq[None, :]
    cos = np.cos(ang).astype(np.float32)
    sin = np.sin(ang).astype(np.float32)
    return cos, np.ascontiguousarray(np.stack([-sin, sin], 1))


def kernel(x, cond_1024, ctx_1024, L0_xcond_ln1_w, L0_xcond_ln1_b, L0_xcond_ln2_w, L0_xcond_ln2_b,
           L0_xcond_ln3_w, L0_xcond_ln3_b, L0_xcond_qkv_w, L0_xcond_sa_out_w, L0_xcond_q_w, L0_xcond_k_w,
           L0_xcond_v_w, L0_xcond_ca_out_w, L0_xcond_ffn_w1, L0_xcond_ffn_b1, L0_xcond_ffn_w2, L0_xcond_ffn_b2):
    import concourse.bacc as bacc
    from concourse.bass_utils import run_bass_kernel_spmd

    a = {n: np.asarray(v) for n, v in locals().items() if n not in ("bacc", "run_bass_kernel_spmd")}
    B, L, D = a["x"].shape
    half = 16
    cos, sin = rope_tables(L, half)
    ln_w = [a[f"L0_xcond_ln{n}_w"].T for n in (1, 2, 3)]
    ln_b = [a[f"L0_xcond_ln{n}_b"].reshape(-1, P).T for n in (1, 2, 3)]
    qkv = a["L0_xcond_qkv_w"].reshape(3, D, D).transpose(0, 2, 1)
    layers = [[*qkv, a["L0_xcond_sa_out_w"].T],
              [a["L0_xcond_q_w"].T, a["L0_xcond_k_w"].T, a["L0_xcond_v_w"].T, a["L0_xcond_ca_out_w"].T]]
    arrays = {
        "x": a["x"],
        "condT": a["cond_1024"].T,
        "ctxT": a["ctx_1024"].transpose(0, 2, 1),
        "lnT": np.stack(ln_w),
        "lnb": np.stack(ln_b, 1),
        "attnT": np.stack([np.stack(m) for m in layers]),
        "w1T": a["L0_xcond_ffn_w1"].T,
        "b1": a["L0_xcond_ffn_b1"].reshape(-1, P).T,
        "w2T": a["L0_xcond_ffn_w2"].T,
        "b2": a["L0_xcond_ffn_b2"],
        "cos": cos,
        "sin": sin,
        "pick": np.tile(np.eye(D // (2 * half) // 2, dtype=np.float32), (2, 1)),
        "ident": np.eye(P, dtype=np.float32),
    }
    arrays = {n: np.ascontiguousarray(v) for n, v in arrays.items()}
    nc = bacc.Bacc("TRN2", target_bir_lowering=False, num_devices=1)
    ins = [nc.dram_tensor(f"in_{n}", v.shape, mybir.dt.from_np(v.dtype), kind="ExternalInput").ap() for n, v in arrays.items()]
    x1, x2 = (nc.dram_tensor(n, (B, L, D), F32, kind="Internal").ap() for n in ("x_after_self", "x_after_cross"))
    out = nc.dram_tensor("out_y", (B, L, D), F32, kind="ExternalOutput").ap()
    block_kernel(nc, *ins, x1, x2, out)
    r = run_bass_kernel_spmd(nc, [{f"in_{n}": v for n, v in arrays.items()}], core_ids=[0])
    return r.results[0]["out_y"]
```

```python
from contextlib import ExitStack

import concourse.bass as bass
import numpy as np
from concourse import mybir

F32 = mybir.dt.float32
F32R = mybir.dt.float32r
ACT = mybir.ActivationFunctionType
ALU = mybir.AluOpType
AX = mybir.AxisListType

P = 128
EPS = 1e-5
ROPE_BASE = 10000.0


class Queue:

    def __init__(self, sem):
        self.sem, self.count, self.items = sem, 0, []

    def put(self, make, *tickets, signal=True):
        self.items.append((tickets, make, self.sem if signal else None, 1))
        self.count += 1 if signal else 0
        return (self.sem, self.count) if signal else None

    def dma(self, make, slot, *tickets):
        slot.count += 16
        self.items.append((tickets, make, slot.sem, 16))
        return (slot.sem, slot.count)

    def wait(self, *tickets):
        self.items.append((tickets, None, None, 0))

    def play(self, eng):
        reached = {}
        for tickets, make, sem, step in self.items:
            for ticket in tickets:
                if ticket is not None and reached.get(id(ticket[0]), 0) < ticket[1]:
                    eng.wait_ge(ticket[0], ticket[1])
                    reached[id(ticket[0])] = ticket[1]
            if make is not None:
                ins = make(eng)
                if sem is not None:
                    ins.then_inc(sem, step)


class Slot:

    def __init__(self, sem):
        self.sem, self.count = sem, 0


class Pace:

    def __init__(self):
        self.now, self.waiting = 0.0, []

    def later(self, delay, step):
        self.waiting.append((self.now + delay, len(self.waiting), step))
        self.waiting.sort(key=lambda w: w[0])

    def spend(self, us):
        end = self.now + us
        while self.waiting and self.waiting[0][0] <= end:
            due, _, step = self.waiting.pop(0)
            self.now = max(self.now, due)
            step()
        self.now = end

    def flush(self):
        while self.waiting:
            self.spend(max(0.0, self.waiting[0][0] - self.now))


def block_kernel(nc, x, condT, ctxT, lnT, lnb, attnT, w1T, b1, w2T, b2, cos, sin, pick, ident_in, x1, x2, out):
    B, L, D = x.shape
    HALF = cos.shape[1]
    HD = 2 * HALF
    H = D // HD
    F = b1.shape[1] * P
    KC = D // P
    T = L // P
    HG = H // 2
    FC = F // P
    SCALE = float(HD) ** -0.5
    ROWS = 3 * HD
    MROWS = ROWS + 2 * HG
    VW = HD + 1
    OH = 4
    N_ITEMS = 2 * B

    with ExitStack() as whole:
        def sem(name):
            return whole.enter_context(nc.semaphore(name))

        def keep(name, shape, dt=F32):
            return whole.enter_context(nc.sbuf_tensor(name, shape, dt))

        ident = keep("ident", [P, P])
        gb = keep("gb", [P, 3, 2 * KC, B])
        neg_half = keep("neg_half", [P, 4])
        w_hi, w_lo = (keep(f"w_{part}", [P, 4 * KC, D], F32R) for part in ("hi", "lo"))
        pe, act, dve, pool, sp = (Queue(sem(n)) for n in ("pe_done", "act_done", "dve_done", "pool_done", "sp_done"))
        slots = {}
        pace = Pace()

        def slot(name):
            if name not in slots:
                slots[name] = Slot(sem(name))
            return slots[name]

        def run(queues):
            with nc.Block() as block:
                @block.tensor
                def _(eng):
                    pe.play(eng)

                @block.scalar
                def _(eng):
                    act.play(eng)

                @block.vector
                def _(eng):
                    dve.play(eng)

                @block.gpsimd
                def _(eng):
                    pool.play(eng)

                @block.sync
                def _(eng):
                    sp.play(eng)
            for q in queues:
                q.items = []

        queues = (pe, act, dve, pool, sp)
        EARLY = 3 * KC

        def hidden_row(k):
            c = k // 2
            if k % 2 == 0:
                return (w1T[:, c * P:(c + 1) * P].rearrange("(k p) f -> p k f", p=P),
                        lambda raw: raw.rearrange("p (k f) -> p k f", k=KC))
            return w2T[c * P:(c + 1) * P, :], lambda raw: raw

        with ExitStack() as stage:
            def sb(name, shape, dt=F32):
                return stage.enter_context(nc.sbuf_tensor(name, shape, dt))

            MATS = ("q", "k", "v", "o")
            NW = 4
            w_raw = sb("w_raw", [P, NW, D])
            ln_b = sb("ln_b", [P, 3, 2 * KC])
            cond_sb = sb("cond_sb", [P, KC, B])
            cos_sb = sb("cos_sb", [P, T, HALF])
            pick_sb = sb("pick_sb", [P, HG])
            sin_sb = sb("sin_sb", [P, T, 2, HALF])
            xn = sb("xn", [P, T, D])
            res = sb("res", [P, T, D])
            stats = sb("stats", [P, T, 6])
            mv = sb("mv", [P, T, 2])
            rstd_in = sb("rstd_in", [P, T])
            rstd = sb("rstd", [P, T])
            xT = sb("xT", [P, KC, L])
            x_hi = sb("x_hi", [P, KC, L], F32R)
            x_lo = sb("x_lo", [P, KC, L], F32R)
            ctx_hi = sb("ctx_hi", [P, KC, L], F32R)
            ctx_lo = sb("ctx_lo", [P, KC, L], F32R)
            rope_c = [sb(f"rope_c{i}", [P, D]) for i in range(2)]
            rope_s = sb("rope_s", [P, D])
            rot_hi, rot_lo = ({m: sb(f"{m}_{part}", [P, KC, L], F32R) for m in "qk"} for part in ("hi", "lo"))
            CH = P // HD
            NG = 3
            qT = sb("qT", [MROWS, NG, HG, L], F32R)
            kT = sb("kT", [MROWS, NG, HG, L], F32R)
            NV = 3
            v_sb = [sb(f"v_sb{i}", [P, T, H, VW]) for i in range(NV)]
            neg_max = [sb(f"neg_max{i}", [P, T, HG]) for i in range(2)]
            max_parts = sb("max_parts", [P, T, 2, HG])
            maxT = sb("maxT", [2 * HG, L], F32R)
            NP = 3
            prob = sb("prob", [P, NP, T, L])
            rden = sb("rden", [P, OH, T])
            o_sb = sb("o_sb", [P, T, D])
            o_hi = sb("o_hi", [P, KC, L], F32R)
            o_lo = sb("o_lo", [P, KC, L], F32R)

            def psum(name, n):
                return stage.enter_context(nc.psum_tensor(name, [P, n, 512], F32))

            ps_s = psum("ps_s", 2)
            ps_t = psum("ps_t", 2)
            NB = 4
            ps_g = psum("ps_g", NB)

            GEMM = 3 * KC * 0.216

            loaded_small = {
                "cond": sp.dma(lambda e: e.dma_start(cond_sb[:, :, :], condT.rearrange("(c p) b -> p c b", p=P)), slot("cond_in")),
                "lnb": sp.dma(lambda e: e.dma_start(ln_b[:, :, :], lnb), slot("lnb_in")),
                "ident": sp.dma(lambda e: e.dma_start(ident[:, :], ident_in), slot("ident_in")),
                "pick": sp.dma(lambda e: e.dma_start(pick_sb[ROWS:MROWS, :], pick), slot("pick_in")),
                "cos": sp.dma(lambda e: e.dma_start(cos_sb[:, :, :], cos.rearrange("(t p) d -> p t d", p=P)), slot("cos_in")),
                "sin": sp.dma(lambda e: e.dma_start(sin_sb[:, :, :, :], sin.rearrange("(t p) s d -> p t s d", p=P)), slot("sin_in")),
            }

            last = {}

            free_banks = [(n, None) for n in range(NB)]

            def take_bank():
                return free_banks.pop(0)

            def give_bank(n, reader):
                free_banks.append((n, reader))

            x_loaded, res_loaded, stored = {}, {}, {}

            def load_x(i):
                layer, b = divmod(i, B)
                src = x if layer == 0 else x1
                x_loaded[i] = sp.dma(lambda e: e.dma_start(xn[:, :, :], src[b].rearrange("(t p) d -> p t d", p=P)),
                                     slot("x_in"), last.get("xn_read"), stored.get((layer - 1, b)))

            def load_res(i):
                layer, b = divmod(i, B)
                src = x if layer == 0 else x1
                res_loaded[i] = sp.dma(lambda e: e.dma_start(res[:, :, :], src[b].rearrange("(t p) d -> p t d", p=P)),
                                       slot("res_in"), stored.get(divmod(i - 1, B)), stored.get((layer - 1, b)))

            raw_free = [None] * NW
            raw_turn = [0]
            row_free = [None] * (4 * KC)
            row_ready = {}

            def load_row(name, row, src, view):
                r = raw_turn[0] % NW
                raw_turn[0] += 1
                got = sp.dma(lambda e: e.dma_start(view(w_raw[:, r, :]), src), slot(f"w_raw_in{r}"), raw_free[r])

                def split():
                    hi = act.put(lambda e: e.activation(w_hi[:, row, :], w_raw[:, r, :], ACT.Copy), got, row_free[row])
                    lo = dve.put(lambda e: e.tensor_tensor(
                        w_lo[:, row, :], w_raw[:, r, :], w_hi[:, row, :].bitcast(F32), ALU.subtract), hi)
                    raw_free[r] = lo
                    row_ready[name] = lo
                return split

            rows_to_load = []
            loading = [0]

            def load_rows():
                while rows_to_load and loading[0] < NW:
                    split = load_row(*rows_to_load.pop(0))
                    loading[0] += 1

                    def finish(split=split):
                        split()
                        loading[0] -= 1
                        load_rows()
                    pace.later(2.5, finish)

            def load_weight(layer, m):
                n = MATS.index(m)
                rows_to_load.extend(((layer, m, c), n * KC + c, attnT[layer, n, c * P:(c + 1) * P, :], lambda raw: raw)
                                    for c in range(KC))
                load_rows()

            gb_ready = {}

            def modulation(n):
                s = {}

                def load(c):
                    r = 2 * (c % (NW // 2))
                    s["got", c] = sp.dma(lambda e: e.dma_start(
                        w_raw[:, r:r + 2, :].rearrange("p a d -> p (a d)"), lnT[n, c * P:(c + 1) * P, :]),
                        slot(f"w_raw_in{r}"), *raw_free[r:r + 2])

                def start():
                    assert not loading[0]
                    for c in range(NW // 2):
                        load(c)

                def chunk(c):
                    if c == 0:
                        s["bank"] = take_bank()
                    bank, free = s["bank"]
                    r = 2 * (c % (NW // 2))
                    for m in range(2 * KC):
                        row = w_raw[:, r + m // KC, (m % KC) * P:(m % KC + 1) * P]
                        done = pe.put(lambda e, m=m, row=row: e.matmul(
                            ps_g[:, bank, m * B:(m + 1) * B], row, cond_sb[:, c, :], start=c == 0 and m == 0,
                            stop=c == KC - 1, skip_group_check=True),
                            s["got", c], loaded_small["cond"], free, signal=m == 2 * KC - 1)
                    raw_free[r:r + 2] = [done, done]
                    if c + NW // 2 < KC:
                        load(c + NW // 2)
                    if c == KC - 1:
                        added = dve.put(lambda e: e.tensor_tensor(
                            gb[:, n, :, :], ps_g[:, bank, 0:2 * KC * B].rearrange("p (m b) -> p m b", b=B),
                            ln_b[:, n, :].unsqueeze(2).broadcast_to([P, 2 * KC, B]), ALU.add), done, loaded_small["lnb"])
                        give_bank(bank, added)
                        gb_ready[n] = dve.put(lambda e: e.tensor_scalar(
                            gb[:, n, 0:KC, :], gb[:, n, 0:KC, :], 1.0, None, ALU.add), added)
                return start, [(1.0, lambda c=c: chunk(c)) for c in range(KC)]

            ones = [dve.put(lambda e, i=i: e.memset(v_sb[i][:, :, :, HD:VW], 1.0)) for i in range(NV)]
            dve.put(lambda e: e.memset(neg_half[:, :], -0.5))

            group_ready = {}
            weighed_last = {}
            v_ready, v_done = {}, {}
            x_ready, ctx_ready = {}, {}
            stacked = {}
            rot_free = {"q": (), "k": ()}
            stacking = []
            rope_turn = [0]
            rope_free = [None, None]

            def norm(i):
                for t in range(T):
                    seen = dve.put(lambda e, t=t: e.bn_stats(stats[:, t, :], xn[:, t, :]), x_loaded[i])
                for t in range(T):
                    agg = dve.put(lambda e, t=t: e.bn_aggr(mv[:, t, :], stats[:, t, :]), seen)
                shifted = dve.put(lambda e: e.tensor_scalar(rstd_in[:, :], mv[:, :, 1], EPS, None, ALU.add), agg)
                root = pool.put(lambda e: e.tensor_tensor(rstd[:, :], rstd_in[:, :], neg_half[:, 0:T], ALU.pow), shifted)

                def scale():
                    for t in range(T):
                        last["xn"] = dve.put(lambda e, t=t: e.tensor_scalar(
                            xn[:, t, :], xn[:, t, :], mv[:, t, 0:1], rstd[:, t:t + 1], ALU.subtract, ALU.mult), root)
                pace.later(2.5, scale)

            def turn_x(i, half):
                layer, b = divmod(i, B)
                n, free = take_bank()
                for c in range(2):
                    for t in range(T):
                        k = 2 * half + c
                        done = pe.put(lambda e, c=c, t=t, k=k: e.transpose(
                            ps_g[:, n, c * L + t * P:c * L + (t + 1) * P], xn[:, t, k * P:(k + 1) * P], ident[:, :]),
                            last["xn"], loaded_small["ident"], free)
                last["xn_read"] = done
                if half == 1 and i + 1 < N_ITEMS:
                    load_x(i + 1)
                for c in range(2):
                    k = 2 * half + c
                    full = act.put(lambda e, c=c, k=k: e.activation(
                        xT[:, k, :], ps_g[:, n, c * L:(c + 1) * L], ACT.Identity,
                        bias=gb[:, layer, KC + k, b:b + 1], scale=gb[:, layer, k, b:b + 1]),
                        done, gb_ready[layer], last.get("xT"))
                give_bank(n, full)
                ks = slice(2 * half, 2 * half + 2)
                hi = act.put(lambda e: e.activation(x_hi[:, ks, :], xT[:, ks, :], ACT.Copy), full, last.get("x_split"))

                def low():
                    done = dve.put(lambda e: e.tensor_tensor(
                        x_lo[:, ks, :], xT[:, ks, :], x_hi[:, ks, :].bitcast(F32), ALU.subtract), hi)
                    x_ready[i, half] = done
                    if layer == 0:
                        ctx_ready[i, half] = done
                    if half == 1:
                        last["xT"] = done
                pace.later(1.5, low)

            def split_ctx(i):
                b = i % B
                full = sp.dma(lambda e: e.dma_start(xT[:, :, :], ctxT[b].rearrange("(c p) l -> p c l", p=P)), slot("ctx_in"),
                              last["xT"])
                pieces = [slice(2 * half, 2 * half + 2) for half in range(2)]

                def split():
                    his = [act.put(lambda e, ks=ks: e.activation(ctx_hi[:, ks, :], xT[:, ks, :], ACT.Copy), full, last.get("ctx_split"))
                           for ks in pieces]

                    def low():
                        for half, (ks, hi) in enumerate(zip(pieces, his)):
                            ctx_ready[i, half] = dve.put(lambda e, ks=ks: e.tensor_tensor(
                                ctx_lo[:, ks, :], xT[:, ks, :], ctx_hi[:, ks, :].bitcast(F32), ALU.subtract), hi)
                        last["xT"] = ctx_ready[i, 1]
                    pace.later(1.0, low)
                pace.later(5.2, split)

            def project(layer, m, t, hi, lo, ready, after, known=lambda: True):
                row = MATS.index(m) * KC
                s = {}

                def chunk(c):
                    if c == 0:
                        s["bank"] = take_bank()
                    n, free = s["bank"]
                    for j, (a, w) in enumerate(((hi, w_hi), (hi, w_lo), (lo, w_hi))):
                        done = pe.put(lambda e, a=a, w=w, j=j: e.matmul(
                            ps_g[:, n, :], a[:, c, t * P:(t + 1) * P], w[:, row + c, :],
                            start=c == 0 and j == 0, stop=c == KC - 1 and j == 2),
                            ready(c // 2), row_ready[layer, m, c], free, signal=j == 2)
                    row_free[row + c] = done
                    if c == KC - 1:
                        after(n, done)
                for c in range(KC):
                    yield GEMM / KC, lambda c=c: chunk(c), lambda c=c: (layer, m, c) in row_ready and known()

            def rope_and_turn(i, m, t, n, done):
                r = rope_turn[0] % 2
                rope_turn[0] += 1
                turned_out = rope_c[r]
                free_out = rope_free[r]
                assert free_out != "taken"
                rope_free[r] = "taken"
                dve.put(lambda e: e.tensor_tensor(
                    turned_out[:, :].rearrange("p (h d) -> p h d", d=HALF), ps_g[:, n, :].rearrange("p (h d) -> p h d", d=HALF),
                    cos_sb[:, t, :].unsqueeze(1).broadcast_to([P, 2 * H, HALF]), ALU.mult),
                    done, free_out, loaded_small["cos"])
                rotated = dve.put(lambda e: e.tensor_tensor(
                    rope_s[:, :].rearrange("p (h s d) -> p h s d", s=2, d=HALF),
                    ps_g[:, n, :].rearrange("p (h s d) -> p h s d", s=2, d=HALF)[:, :, ::-1, :],
                    sin_sb[:, t, :, :].unsqueeze(1).broadcast_to([P, H, 2, HALF]), ALU.mult),
                    last.get("rope_s"), loaded_small["sin"])
                give_bank(n, rotated)
                total = pool.put(lambda e: e.tensor_tensor(turned_out[:, :], turned_out[:, :], rope_s[:, :], ALU.add), rotated)
                last["rope_s"] = total

                def turn():
                    if i and stacked.get((i - 1, m), 0) < 2:
                        pace.later(0.5, turn)
                        return
                    b, free = take_bank()
                    for c in range(KC):
                        done = pe.put(lambda e, c=c: e.transpose(
                            ps_g[:, b, c * P:(c + 1) * P], turned_out[:, c * P:(c + 1) * P], ident[:, :]),
                            total, free, signal=c == KC - 1)
                    rope_free[r] = done
                    got = ps_g[:, b, :].rearrange("p (c l) -> p c l", l=P)
                    mine = slice(t * P, (t + 1) * P)
                    hi = act.put(lambda e: e.activation(rot_hi[m][:, :, mine], got, ACT.Copy), done, *rot_free[m])
                    lo = dve.put(lambda e: e.tensor_tensor(
                        rot_lo[m][:, :, mine], got, rot_hi[m][:, :, mine].bitcast(F32), ALU.subtract), hi, *rot_free[m])
                    give_bank(b, lo)
                    if t == T - 1:
                        for g in range(2):
                            stack_set(2 * i + g, m, lo)
                pace.later(3.4, turn)

            def stack_set(G, m, ready):
                dst = qT if m == "q" else kT
                parts = (rot_hi, rot_hi, rot_lo) if m == "q" else (rot_hi, rot_lo, rot_hi)
                chunks = slice((G % 2) * HG // CH, (G % 2 + 1) * HG // CH)
                left = [3 * CH]

                def start(j, s):
                    copied = sp.dma(lambda e: e.dma_start(
                        dst[s * HD:(s + 1) * HD, G % NG, j::CH, :].bitcast(F32),
                        parts[s][m][j * HD:(j + 1) * HD, chunks, :].bitcast(F32)),
                        slot(f"stack_{m}{G % 2}"), ready, weighed_last.get(before(G, j)))
                    left[0] -= 1
                    if not left[0]:
                        group_ready.setdefault(G, []).append(copied)
                        rot_free[m] = (*rot_free[m], copied) if G % 2 else (copied,)
                        stacked[G // 2, m] = stacked.get((G // 2, m), 0) + 1
                for j in range(CH):
                    for s in range(3):
                        stacking.append((G, j, lambda j=j, s=s: start(j, s)))
                stacking.sort(key=lambda entry: entry[:2])

            def before(G, j):
                return (G - NG) * HG + j + HG - CH

            def stack_some(n):
                while n and stacking and (stacking[0][0] < NG or before(*stacking[0][:2]) in weighed_last):
                    stacking.pop(0)[2]()
                    n -= 1

            def qk(i, m, t):
                layer = i // B
                if m == "k" and layer:
                    hi, lo, ready = ctx_hi, ctx_lo, lambda half: ctx_ready[i, half]
                else:
                    hi, lo, ready = x_hi, x_lo, lambda half: x_ready[i, half]

                def after(n, done):
                    rope_and_turn(i, m, t, n, done)
                return project(layer, m, t, hi, lo, ready, after)

            def v(i, t):
                layer = i // B
                hi, lo = (ctx_hi, ctx_lo) if layer else (x_hi, x_lo)

                def after(n, done):
                    v_ready[i] = act.put(lambda e: e.activation(
                        v_sb[i % NV][:, t, :, 0:HD], ps_g[:, n, :].rearrange("p (h d) -> p h d", d=HD), ACT.Copy),
                        done, v_done[i - NV] if i >= NV else None)
                    give_bank(n, v_ready[i])
                    last["x_split"] = last["ctx_split"] = done
                return project(layer, "v", t, hi, lo, lambda half: ctx_ready[i, half], after, lambda: (i, 1) in ctx_ready)

            score_reader = [None, None]
            probT_reader = [None, None]
            prob_reader = [None] * NP
            out_bank = [None]
            max_ready = {}
            o_ready, maxes_read, mixed = {}, {}, {}

            def scores(G, j):
                n = j % 2
                ring = G % NG
                for t in range(T):
                    done = pe.put(lambda e, t=t: e.matmul(
                        ps_s[:, n, t * L:(t + 1) * L], qT[0:ROWS, ring, j, t * P:(t + 1) * P], kT[0:ROWS, ring, j, :],
                        start=True, stop=True), *group_ready[G], score_reader[n], signal=t == T - 1)
                score_reader[n] = dve.put(lambda e: e.tensor_reduce(
                    neg_max[G % 2][:, :, j], ps_s[:, n, :].rearrange("p (t l) -> p t l", l=L), AX.X, ALU.max, negate=True),
                    done, maxes_read.get(G - 2))
                if j == HG - 1:
                    found = score_reader[n]
                    parts = max_parts

                    def halve():
                        hi = dve.put(lambda e: e.tensor_copy(parts[:, :, 0, :].bitcast(F32R), neg_max[G % 2][:, :, :]),
                                     found, last.get("max_parts"))
                        maxes_read[G] = dve.put(lambda e: e.tensor_tensor(
                            parts[:, :, 1, :], neg_max[G % 2][:, :, :], parts[:, :, 0, :], ALU.subtract), hi)
                    pace.later(0.0, halve)
                    pace.later(2.6, lambda: spread_max(G))

            def spread_max(G):
                n, free = take_bank()
                for t in range(T):
                    done = pe.put(lambda e, t=t: e.transpose(
                        ps_g[0:2 * HG, n, t * P:(t + 1) * P], max_parts[:, t, :, :].rearrange("p s h -> p (s h)"), ident[:, :]),
                        maxes_read[G], free, signal=t == T - 1)
                last["max_parts"] = done
                copied = act.put(lambda e: e.activation(maxT[:, :], ps_g[0:2 * HG, n, 0:L], ACT.Copy), done, last.get("maxT"))
                give_bank(n, copied)
                last["maxT"] = max_ready[G] = act.dma(lambda e: e.dma_start(
                    qT[ROWS:MROWS, G % NG, :, :].bitcast(F32),
                    maxT[:, :].bitcast(F32).unsqueeze(1).broadcast_to([2 * HG, HG, L])), slot("max_in"), copied)

            def weigh(G, j):
                n, p = j % 2, (G * HG + j) % NP
                ring = G % NG
                for t in range(T):
                    done = pe.put(lambda e, t=t: e.matmul(
                        ps_t[:, n, t * L:(t + 1) * L], kT[:, ring, j, t * P:(t + 1) * P], qT[:, ring, j, :],
                        start=True, stop=True), max_ready[G], *ones, probT_reader[n], signal=t == T - 1)
                weighed_last[G * HG + j] = done
                probT_reader[n] = act.put(lambda e: e.activation(
                    prob[:, p, :, :].rearrange("p t l -> p (t l)"), ps_t[:, n, :], ACT.Exp, scale=SCALE),
                    done, prob_reader[p])
                return probT_reader[n]

            def mix(G, j, weighed):
                i, g = divmod(G, 2)
                h = g * HG + j
                p = (G * HG + j) % NP
                o = j % OH
                base = o * T * VW
                if o == 0:
                    out_bank[0] = take_bank()
                n, free = out_bank[0]
                for t in range(T):
                    for k in range(T):
                        done = pe.put(lambda e, t=t, k=k: e.matmul(
                            ps_g[:, n, base + t * VW:base + (t + 1) * VW], prob[:, p, k, t * P:(t + 1) * P],
                            v_sb[i % NV][:, k, h, :], start=k == 0, stop=k == T - 1),
                            weighed, v_ready[i], *ones, free, signal=(t, k) == (T - 1, T - 1))
                prob_reader[p] = done
                mixed[i] = h + 1
                if h == H - 1:
                    v_done[i] = done
                if o == OH - 1:
                    got = ps_g[:, n, 0:OH * T * VW].rearrange("p (h t w) -> p h t w", t=T, w=VW)
                    inv = dve.put(lambda e: e.reciprocal(rden[:, :, :], got[:, :, :, HD]), done, last.get("rden_read"))
                    for t in range(T):
                        o_ready[i] = dve.put(lambda e, t=t: e.tensor_tensor(
                            o_sb[:, t, (h - OH + 1) * HD:(h + 1) * HD].rearrange("p (h d) -> p h d", d=HD),
                            got[:, :, t, 0:HD], rden[:, :, t].unsqueeze(2).broadcast_to([P, OH, HD]), ALU.mult),
                            inv, last.get("o_read"))
                    last["rden_read"] = o_ready[i]
                    give_bank(n, o_ready[i])

            o_split_ready = {}

            def turn_o(i, half):
                assert mixed[i] == H
                n, free = take_bank()
                for c in range(2):
                    k = 2 * half + c
                    for t in range(T):
                        done = pe.put(lambda e, c=c, t=t, k=k: e.transpose(
                            ps_g[:, n, c * L + t * P:c * L + (t + 1) * P], o_sb[:, t, k * P:(k + 1) * P], ident[:, :]),
                            o_ready[i], free, signal=(c, t) == (1, T - 1))
                last["o_read"] = done
                ks = slice(2 * half, 2 * half + 2)
                got = ps_g[:, n, :].rearrange("p (c l) -> p c l", l=L)
                hi = act.put(lambda e: e.activation(o_hi[:, ks, :], got, ACT.Copy), done, last.get("o_split"))
                o_split_ready[i, half] = dve.put(lambda e: e.tensor_tensor(
                    o_lo[:, ks, :], got, o_hi[:, ks, :].bitcast(F32), ALU.subtract), hi)
                give_bank(n, o_split_ready[i, half])

            def out_proj(i, t):
                layer, b = divmod(i, B)

                def after(n, done):
                    added = dve.put(lambda e: e.tensor_tensor(res[:, t, :], ps_g[:, n, :], res[:, t, :], ALU.add),
                                    done, res_loaded[i])
                    give_bank(n, added)
                    last["o_split"] = done
                    if t == T - 1:
                        dst = x1 if layer == 0 else x2
                        stored[layer, b] = sp.dma(lambda e: e.dma_start(
                            dst[b].rearrange("(t p) d -> p t d", p=P), res[:, :, :]), slot("x_out"), added)
                return project(layer, "o", t, o_hi, o_lo, lambda half: o_split_ready[i, half], after)

            def first_step(i):
                if i + 2 < N_ITEMS:
                    yield 0.0, lambda: norm(i + 2)
                if i >= 2:
                    yield from out_proj(i - 2, 1)
                if i + 1 < N_ITEMS:
                    yield from v(i + 1, 0)
                    yield from qk(i + 1, "k", 0)
                    yield from qk(i + 1, "k", 1)
                    yield from qk(i + 1, "q", 0)
                if i == B - 2:
                    yield 0.0, lambda: load_weight(1, "k")
                if i == B + 1:
                    yield 0.0, lambda: load_weight(1, "o")

            def second_step(i):
                if i < 2:
                    start, products = modulation(i + 1)
                    yield 0.0, start
                if i + 1 < N_ITEMS:
                    yield from qk(i + 1, "q", 1)
                    yield from v(i + 1, 1)
                if i == B - 2:
                    yield 0.0, lambda: (load_weight(1, "q"), load_weight(1, "v"))
                if i == N_ITEMS - 2:
                    yield 0.0, first_hidden_rows
                if i >= 1:
                    yield 0.0, lambda: load_res(i - 1)
                outs = [(0.43, lambda: turn_o(i - 1, 0), lambda: mixed[i - 1] == H and mixed.get(i, 0) >= 1),
                        (0.43, lambda: turn_o(i - 1, 1))] if i >= 1 else []
                xs = [(0.43, lambda half=half: turn_x(i + 2, half)) for half in range(2)] if i + 2 < N_ITEMS else []
                for k in range(2):
                    yield from outs[k:k + 1]
                    yield from xs[k:k + 1]
                if xs and i + 2 >= B:
                    yield 0.0, lambda: split_ctx(i + 2), lambda: (i + 2, 1) in x_ready
                if i >= 1:
                    yield from out_proj(i - 1, 0)
                if i < 2:
                    yield from products

            def first_hidden_rows():
                for k in range(EARLY):
                    rows_to_load.append((("ffn", k), k, *hidden_row(k)))
                load_rows()

            def drive(steps):
                for cost, step, *ready in steps:
                    while ready and not ready[0]():
                        pace.spend(0.2)
                    step()
                    pace.spend(cost)
                    for _ in range(3):
                        if stacking and stacking[0][0] == 0:
                            stack_some(1)

            load_x(0)
            norm(0)
            start, products = modulation(0)
            start()
            for _, step in products:
                step()
            for m in ("k", "q", "v", "o"):
                load_weight(0, m)
            pace.spend(3.0)
            for half in range(2):
                turn_x(0, half)
            pace.spend(2.5)
            norm(1)
            for r in range(NG):
                ones.append(dve.put(lambda e, r=r: e.tensor_copy(
                    kT[ROWS:MROWS, r, :, :], pick_sb[ROWS:MROWS, :].unsqueeze(2).broadcast_to([2 * HG, HG, L])),
                    loaded_small["pick"]))
            for m in "kq":
                for t in range(T):
                    drive(qk(0, m, t))
            for t in range(T):
                drive(v(0, t))
            while stacking and stacking[0][0] == 0:
                stack_some(1)
            for half in range(2):
                turn_x(1, half)
            pace.spend(2.0)

            LAG = 3
            N_HEADS = N_ITEMS * H
            weighed = {}

            def head(n):
                return divmod(n, HG)

            def fill_some(fill, state, goal):
                while fill and state[0] + fill[0][0] / 2 <= goal and (len(fill[0]) < 3 or fill[0][2]()):
                    cost, step = fill.pop(0)[:2]
                    step()
                    pace.spend(cost)
                    state[0] += cost

            for G in range(2 * N_ITEMS):
                i, g = divmod(G, 2)
                copies = 2 if i == N_ITEMS - 1 else 1
                fill = list(second_step(i) if g else first_step(i))
                total = sum(f[0] for f in fill)
                state = [0.0]
                for j in range(HG):
                    n = G * HG + j
                    if j == 0:
                        assert len(group_ready[G]) == 2
                    scores(G, j)
                    pace.spend(0.21)
                    stack_some(2)
                    fill_some(fill, state, total * (3 * j + 1) / (3 * HG))
                    if n - HG - LAG >= 0:
                        weighed[n - HG - LAG] = weigh(*head(n - HG - LAG))
                        pace.spend(0.21)
                    stack_some(copies)
                    fill_some(fill, state, total * (3 * j + 2) / (3 * HG))
                    if n - HG - LAG - 1 >= 0:
                        k = n - HG - LAG - 1
                        mix(*head(k), weighed.pop(k))
                        pace.spend(0.86)
                    stack_some(copies)
                    fill_some(fill, state, total * (3 * j + 3) / (3 * HG) + (1.0 if j == HG - 1 else 0.0))
                assert not fill
            pace.flush()
            for k in range(N_HEADS - HG - LAG, N_HEADS + 1):
                if k < N_HEADS:
                    weighed[k] = weigh(*head(k))
                    pace.spend(0.21)
                if k - 1 >= N_HEADS - HG - LAG - 1:
                    mix(*head(k - 1), weighed.pop(k - 1))
                    pace.spend(0.86)
            drive(out_proj(N_ITEMS - 2, 1))
            load_res(N_ITEMS - 1)
            for half in range(2):
                turn_o(N_ITEMS - 1, half)
            for t in range(T):
                drive(out_proj(N_ITEMS - 1, t))
            pace.flush()
            run(queues)

        with ExitStack() as stage:
            def sb(name, shape, dt=F32):
                return stage.enter_context(nc.sbuf_tensor(name, shape, dt))

            U = 4 * P
            UT = U // P
            NU = B * L // U
            more_hi, more_lo = (sb(f"f_w_{part}", [P, 2 * FC - 4 * KC, D], F32R) for part in ("hi", "lo"))
            place = {}
            for k in range(2 * FC):
                place[1 + k % 2, k // 2] = (w_hi[:, k, :], w_lo[:, k, :]) if k < 4 * KC else (more_hi[:, k - 4 * KC, :], more_lo[:, k - 4 * KC, :])
            NR = 4
            raw = [sb(f"f_raw{i}", [P, D]) for i in range(NR)]
            b1_sb = sb("b1_sb", [P, FC])
            b2_sb = sb("b2_sb", [P, D])
            xn = sb("f_xn", [P, UT, D])
            res = sb("f_res", [P, UT, D])
            stats = sb("f_stats", [P, UT, 6])
            mv = sb("f_mv", [P, UT, 2])
            rstd_in = sb("f_rstd_in", [P, UT])
            rstd = sb("f_rstd", [P, UT])
            half_sb = sb("f_half", [P, UT])
            xT = sb("f_xT", [P, U])
            x_hi = [sb(f"f_x_hi{i}", [P, KC, U], F32R) for i in range(2)]
            x_lo = [sb(f"f_x_lo{i}", [P, KC, U], F32R) for i in range(2)]
            NH = 2
            h_sb = [sb(f"h_sb{i}", [P, U]) for i in range(2)]
            h_hi = [sb(f"h_hi{i}", [P, U], F32R) for i in range(NH)]
            h_lo = [sb(f"h_lo{i}", [P, U], F32R) for i in range(NH)]

            ps_y = stage.enter_context(nc.psum_tensor("ps_y", [P, UT, 512], F32))
            ps_h = stage.enter_context(nc.psum_tensor("ps_h", [P, 2, 512], F32))
            ps_x = stage.enter_context(nc.psum_tensor("ps_x", [P, 2, 512], F32))

            sp_b = [sp.dma(lambda e: e.dma_start(b1_sb[:, :], b1), slot("b1_in")),
                    sp.dma(lambda e: e.dma_start(b2_sb[:, :], b2.partition_broadcast(P)), slot("b2_in"))]
            half_set = dve.put(lambda e: e.memset(half_sb[:, :], -0.5))
            state = {"xn_read": None, "xT_read": None, "bank": [None, None], "turn": 0, "sent": ()}
            x_loaded, res_loaded = {}, {}

            def load(u, dst, name, *free):
                per = U // L
                return [sp.dma(lambda e, j=j: e.dma_start(
                    dst[:, j * T:(j + 1) * T, :], x2[u * per + j].rearrange("(t p) d -> p t d", p=P)),
                    slot(f"{name}{j}"), *free) for j in range(per)]

            x_loaded[0] = load(0, xn, "f_x_in")
            w_ready = {(1 + k % 2, k // 2): row_ready["ffn", k] for k in range(EARLY)}
            f_raw_free = [None] * NR
            raw_loaded = {}

            def load_row(k):
                r = k % NR
                src, view = hidden_row(k)
                raw_loaded[k] = sp.dma(lambda e: e.dma_start(view(raw[r][:, :]), src), slot(f"f_raw_in{r}"), f_raw_free[r])

            def split_row(k):
                r = k % NR
                w_h, w_l = place[list(place)[k]]
                hi = act.put(lambda e: e.activation(w_h, raw[r][:, :], ACT.Copy), raw_loaded[k])
                w_ready[list(place)[k]] = f_raw_free[r] = dve.put(
                    lambda e: e.tensor_tensor(w_l, raw[r][:, :], w_h.bitcast(F32), ALU.subtract), hi)
                if k + NR < len(place):
                    load_row(k + NR)

            for k in range(EARLY, EARLY + NR):
                load_row(k)

            x_split_read = [None, None]
            x_ready, res_ready = {}, {}

            def norm_unit(u):
                for t in range(UT):
                    dve.put(lambda e, t=t: e.bn_stats(stats[:, t, :], xn[:, t, :]), *x_loaded[u])
                s = (dve.sem, dve.count)
                for t in range(UT):
                    a = dve.put(lambda e, t=t: e.bn_aggr(mv[:, t, :], stats[:, t, :]), s)
                shifted = dve.put(lambda e: e.tensor_scalar(rstd_in[:, :], mv[:, :, 1], EPS, None, ALU.add), a)
                root = pool.put(lambda e: e.tensor_tensor(rstd[:, :], rstd_in[:, :], half_sb[:, :], ALU.pow), shifted, half_set)
                for t in range(UT):
                    state["xn"] = dve.put(lambda e, t=t: e.tensor_scalar(
                        xn[:, t, :], xn[:, t, :], mv[:, t, 0:1], rstd[:, t:t + 1], ALU.subtract, ALU.mult), root)

            def residual(u):
                loaded = load(u, res, "f_res_in", *state["sent"])
                for t in range(UT):
                    res_ready[u] = pool.put(lambda e, t=t: e.tensor_tensor(res[:, t, :], res[:, t, :], b2_sb[:, :], ALU.add),
                                            *loaded, sp_b[1])

            def turn_unit(u, k):
                n = state["turn"] % 2
                state["turn"] += 1
                for t in range(UT):
                    done = pe.put(lambda e, t=t: e.transpose(
                        ps_x[:, n, t * P:(t + 1) * P], xn[:, t, k * P:(k + 1) * P], ident[:, :]),
                        state["xn"], state["bank"][n], signal=t == UT - 1)
                state["xn_read"] = done
                per = U // L
                for j in range(per):
                    b = u * per + j
                    full = act.put(lambda e, j=j, b=b: e.activation(
                        xT[:, j * L:(j + 1) * L], ps_x[:, n, j * L:(j + 1) * L], ACT.Identity,
                        bias=gb[:, 2, KC + k, b:b + 1], scale=gb[:, 2, k, b:b + 1]), done, state["xT_read"])
                state["bank"][n] = full
                hi = act.put(lambda e: e.activation(x_hi[u % 2][:, k, :], xT[:, :], ACT.Copy), full, x_split_read[u % 2])
                x_ready[u] = dve.put(lambda e: e.tensor_tensor(
                    x_lo[u % 2][:, k, :], xT[:, :], x_hi[u % 2][:, k, :].bitcast(F32), ALU.subtract), hi, x_split_read[u % 2])
                state["xT_read"] = x_ready[u]

            h_reader = [None] * NH
            ps_h_reader = [None, None]
            h_ready = {}
            hidden = [0]

            def up(u, c):
                a = hidden[0]
                hidden[0] += 1
                n, r, f = a % 2, a % NH, a % 2
                w_h, w_l = place[1, c]
                steps = [(w, xx, k) for k in range(KC) for w, xx in ((w_h, x_hi[u % 2]), (w_l, x_hi[u % 2]), (w_h, x_lo[u % 2]))]
                for j, (w, xx, k) in enumerate(steps):
                    done = pe.put(lambda e, w=w, xx=xx, k=k, j=j: e.matmul(
                        ps_h[:, n, :], w[:, k * P:(k + 1) * P], xx[:, k, :], start=j == 0, stop=j == len(steps) - 1),
                        x_ready[u], w_ready[1, c], ps_h_reader[n], signal=j == len(steps) - 1)
                if c == FC - 1:
                    x_split_read[u % 2] = done
                g = act.put(lambda e: e.activation(h_sb[f][:, :], ps_h[:, n, :], ACT.Gelu, bias=b1_sb[:, c:c + 1]),
                            done, sp_b[0], state.get(("h", f)))
                ps_h_reader[n] = g
                hi = act.put(lambda e: e.activation(h_hi[r][:, :], h_sb[f][:, :], ACT.Copy), g, h_reader[r])
                lo = dve.put(lambda e: e.tensor_tensor(h_lo[r][:, :], h_sb[f][:, :], h_hi[r][:, :].bitcast(F32), ALU.subtract),
                             hi, h_reader[r])
                state["h", f] = lo
                h_ready[u, c] = (r, lo)

            y_reader = [None] * UT

            def down(u, c):
                r, ready = h_ready[u, c]
                w_h, w_l = place[2, c]
                for t in range(UT):
                    for j, (a, w) in enumerate(((h_hi[r], w_h), (h_hi[r], w_l), (h_lo[r], w_h))):
                        done = pe.put(lambda e, t=t, a=a, w=w, j=j: e.matmul(
                            ps_y[:, t, :], a[:, t * P:(t + 1) * P], w,
                            start=c == 0 and j == 0, stop=c == FC - 1 and j == 2),
                            ready, w_ready[2, c], y_reader[t] if c == 0 else None, signal=j == 2)
                    if c == FC - 1:
                        y_reader[t] = dve.put(lambda e, t=t: e.tensor_tensor(res[:, t, :], ps_y[:, t, :], res[:, t, :], ALU.add),
                                              done, res_ready[u])
                h_reader[r] = done
                if c == FC - 1:
                    per = U // L
                    state["sent"] = [sp.dma(lambda e, j=j: e.dma_start(
                        out[u * per + j].rearrange("(t p) d -> p t d", p=P), res[:, j * T:(j + 1) * T, :]),
                        slot(f"f_x_out{j}"), y_reader[(j + 1) * T - 1]) for j in range(per)]
                    if u + 1 < NU:
                        residual(u + 1)
                    else:
                        sp.wait(*state["sent"])

            norm_unit(0)
            residual(0)
            for k in range(KC):
                turn_unit(0, k)
            x_loaded[1] = load(1, xn, "f_x_in", state["xn_read"])
            split_next = EARLY
            LAG = 1
            chunks = [(u, c) for u in range(NU) for c in range(FC)]
            for n in range(len(chunks) + LAG):
                if n < len(chunks):
                    u, c = chunks[n]
                    up(u, c)
                    if u == 0:
                        while split_next < min(EARLY + 2 * c + 2, len(place)):
                            split_row(split_next)
                            split_next += 1
                    if u + 1 < NU:
                        if c == FC - KC - 4:
                            norm_unit(u + 1)
                        if FC - KC - 1 <= c < FC - 1:
                            turn_unit(u + 1, c - (FC - KC - 1))
                        if c == FC - 1 and u + 2 < NU:
                            x_loaded[u + 2] = load(u + 2, xn, "f_x_in", state["xn_read"])
                if n >= LAG:
                    down(*chunks[n - LAG])
            run(queues)


def rope_tables(length, half):
    inv_freq = (1.0 / np.float32(ROPE_BASE) ** (np.arange(half, dtype=np.float32) / np.float32(half))).astype(np.float32)
    ang = np.arange(length, dtype=np.float32)[:, None] * inv_freq[None, :]
    cos = np.cos(ang).astype(np.float32)
    sin = np.sin(ang).astype(np.float32)
    return cos, np.ascontiguousarray(np.stack([-sin, sin], 1))


def kernel(x, cond_1024, ctx_1024, L0_xcond_ln1_w, L0_xcond_ln1_b, L0_xcond_ln2_w, L0_xcond_ln2_b,
           L0_xcond_ln3_w, L0_xcond_ln3_b, L0_xcond_qkv_w, L0_xcond_sa_out_w, L0_xcond_q_w, L0_xcond_k_w,
           L0_xcond_v_w, L0_xcond_ca_out_w, L0_xcond_ffn_w1, L0_xcond_ffn_b1, L0_xcond_ffn_w2, L0_xcond_ffn_b2):
    import concourse.bacc as bacc
    from concourse.bass_utils import run_bass_kernel_spmd

    a = {n: np.asarray(v) for n, v in locals().items() if n not in ("bacc", "run_bass_kernel_spmd")}
    B, L, D = a["x"].shape
    half = 16
    cos, sin = rope_tables(L, half)
    ln_w = [a[f"L0_xcond_ln{n}_w"].T for n in (1, 2, 3)]
    ln_b = [a[f"L0_xcond_ln{n}_b"].reshape(-1, P).T for n in (1, 2, 3)]
    qkv = a["L0_xcond_qkv_w"].reshape(3, D, D).transpose(0, 2, 1)
    layers = [[*qkv, a["L0_xcond_sa_out_w"].T],
              [a["L0_xcond_q_w"].T, a["L0_xcond_k_w"].T, a["L0_xcond_v_w"].T, a["L0_xcond_ca_out_w"].T]]
    arrays = {
        "x": a["x"],
        "condT": a["cond_1024"].T,
        "ctxT": a["ctx_1024"].transpose(0, 2, 1),
        "lnT": np.stack(ln_w),
        "lnb": np.stack(ln_b, 1),
        "attnT": np.stack([np.stack(m) for m in layers]),
        "w1T": a["L0_xcond_ffn_w1"].T,
        "b1": a["L0_xcond_ffn_b1"].reshape(-1, P).T,
        "w2T": a["L0_xcond_ffn_w2"].T,
        "b2": a["L0_xcond_ffn_b2"],
        "cos": cos,
        "sin": sin,
        "pick": np.tile(np.eye(D // (2 * half) // 2, dtype=np.float32), (2, 1)),
        "ident": np.eye(P, dtype=np.float32),
    }
    arrays = {n: np.ascontiguousarray(v) for n, v in arrays.items()}
    nc = bacc.Bacc("TRN2", target_bir_lowering=False, num_devices=1)
    ins = [nc.dram_tensor(f"in_{n}", v.shape, mybir.dt.from_np(v.dtype), kind="ExternalInput").ap() for n, v in arrays.items()]
    x1, x2 = (nc.dram_tensor(n, (B, L, D), F32, kind="Internal").ap() for n in ("x_after_self", "x_after_cross"))
    out = nc.dram_tensor("out_y", (B, L, D), F32, kind="ExternalOutput").ap()
    block_kernel(nc, *ins, x1, x2, out)
    r = run_bass_kernel_spmd(nc, [{f"in_{n}": v for n, v in arrays.items()}], core_ids=[0])
    return r.results[0]["out_y"]
```
